# Optimizing a Trainium2 kernel written in Bass

```python
import numpy as np
import jax
import jax.numpy as jnp

def _softmax(x, axis=-1):
    return jax.nn.softmax(x, axis=axis)

def _gelu(x):
    return jax.nn.gelu(x, approximate=True)

def _silu(x):
    return jax.nn.silu(x)

def _sigmoid(x):
    return jax.nn.sigmoid(x)

def _layernorm(x, axis=-1, eps=1e-05):
    m = jnp.mean(x, axis=axis, keepdims=True)
    v = jnp.var(x, axis=axis, keepdims=True)
    return (x - m) / jnp.sqrt(v + eps)

def _scatter_add(tgt, idx, src, axis=0):
    return tgt.at[idx].add(src)

def _segment_sum(src, seg, n):
    return jax.ops.segment_sum(src, seg, n)
kernel_name = 'mk_seq_preln_d1_jaxref_r4_5c7816'

def setup_inputs(seed: int=0):
    np.random.seed(seed)
    _w = jnp.asarray

    def _L0_attn_setup():
        import jax, jax.numpy as jnp
        import numpy as np
        B, S, H = (2, 512, 512)
        NH, HD = (16, H // 16)
        WINDOW = 256
        THETA = 10000.0
        EPS = 1e-06

        def rmsnorm(x, w):
            var = jnp.mean(jnp.square(x), axis=-1, keepdims=True)
            return x * jax.lax.rsqrt(var + EPS) * w

        def rope(x, cos, sin):
            d2 = x.shape[-1] // 2
            x1, x2 = (x[..., :d2], x[..., d2:])
            c = cos[None, :, None, :]
            s = sin[None, :, None, :]
            return jnp.concatenate([x1 * c - x2 * s, x2 * c + x1 * s], axis=-1)
        key = jax.random.key(seed)
        k1, k2, k3 = jax.random.split(key, 3)
        sc = 1.0 / np.sqrt(H)
        return {'hidden_states': jax.random.normal(k1, (B, S, H), dtype=jnp.float32), 'Wqkv': jax.random.normal(k2, (H, 3 * H), dtype=jnp.float32) * sc, 'q_norm_w': jnp.ones((H,), dtype=jnp.float32), 'k_norm_w': jnp.ones((H,), dtype=jnp.float32), 'Wo': jax.random.normal(k3, (H, H), dtype=jnp.float32) * sc}
    _L0_attn_in = _L0_attn_setup()

    def _L0_ffn_setup():
        import jax, jax.numpy as jnp
        import numpy as np

        def ternary_quantize(t, threshold, scale):
            return jnp.where(t > threshold, scale, jnp.where(t < -threshold, -scale, 0.0)).astype(t.dtype)
        key = jax.random.key(seed)
        k1, k2, k3 = jax.random.split(key, 3)
        B, S, D = (4, 1024, 512)
        x = jax.random.normal(k1, (B, S, D), dtype=jnp.float32)
        weight = jax.random.normal(k2, (D, D), dtype=jnp.float32) * 0.02
        rram_variation = jax.random.normal(k3, (D, D), dtype=jnp.float32) * 0.05
        return {'x': x, 'weight': weight, 'rram_variation': rram_variation}
    _L0_ffn_in = _L0_ffn_setup()
    _d = {'L0_attn_hidden_states': _L0_attn_in['hidden_states'], 'L0_attn_Wqkv': _L0_attn_in['Wqkv'], 'L0_attn_q_norm_w': _L0_attn_in['q_norm_w'], 'L0_attn_k_norm_w': _L0_attn_in['k_norm_w'], 'L0_attn_Wo': _L0_attn_in['Wo'], 'L0_ffn_weight': _L0_ffn_in['weight'], 'L0_ffn_rram_variation': _L0_ffn_in['rram_variation']}
    _x0 = _d['L0_attn_hidden_states']
    _d['L0_attn_hidden_states'] = jax.random.normal(jax.random.fold_in(jax.random.key(seed), 1), (1, 2048, 512), dtype=_x0.dtype)
    del _x0
    return _d

def reference(L0_attn_hidden_states, L0_attn_Wqkv, L0_attn_q_norm_w, L0_attn_k_norm_w, L0_attn_Wo, L0_ffn_weight, L0_ffn_rram_variation):

    def _L0_attn_ref(hidden_states, Wqkv, q_norm_w, k_norm_w, Wo):
        import jax, jax.numpy as jnp
        import numpy as np
        B, S, H = (2, 512, 512)
        NH, HD = (16, H // 16)
        WINDOW = 256
        THETA = 10000.0
        EPS = 1e-06

        def rmsnorm(x, w):
            var = jnp.mean(jnp.square(x), axis=-1, keepdims=True)
            return x * jax.lax.rsqrt(var + EPS) * w

        def rope(x, cos, sin):
            d2 = x.shape[-1] // 2
            x1, x2 = (x[..., :d2], x[..., d2:])
            c = cos[None, :, None, :]
            s = sin[None, :, None, :]
            return jnp.concatenate([x1 * c - x2 * s, x2 * c + x1 * s], axis=-1)
        b, s, h = hidden_states.shape
        qkv = hidden_states @ Wqkv
        q, k, v = jnp.split(qkv, 3, axis=-1)
        q = rmsnorm(q, q_norm_w)
        k = rmsnorm(k, k_norm_w)
        q = q.reshape(b, s, NH, HD)
        k = k.reshape(b, s, NH, HD)
        v = v.reshape(b, s, NH, HD)
        inv_freq = 1.0 / THETA ** (jnp.arange(0, HD, 2, dtype=jnp.float32) / HD)
        freqs = jnp.arange(s, dtype=jnp.float32)[:, None] * inv_freq[None, :]
        cos, sin = (jnp.cos(freqs), jnp.sin(freqs))
        q = rope(q, cos, sin)
        k = rope(k, cos, sin)
        q_idx = jnp.arange(s)[:, None]
        k_idx = jnp.arange(s)[None, :]
        mask = (q_idx >= k_idx) & (q_idx - k_idx <= WINDOW - 1)
        scale = 1.0 / np.sqrt(HD)
        scores = jnp.einsum('bqhd,bkhd->bhqk', q, k) * scale
        scores = jnp.where(mask[None, None, :, :], scores, jnp.float32(-jnp.inf))
        probs = jax.nn.softmax(scores, axis=-1)
        o = jnp.einsum('bhqk,bkhd->bqhd', probs, v).reshape(b, s, h)
        return o @ Wo

    def _L0_ffn_ref(x, weight, rram_variation):
        import jax, jax.numpy as jnp
        import numpy as np

        def ternary_quantize(t, threshold, scale):
            return jnp.where(t > threshold, scale, jnp.where(t < -threshold, -scale, 0.0)).astype(t.dtype)
        TH_X, SC_X = (0.33, 0.5)
        TH_W, SC_W = (0.2, 0.6)
        x_q = ternary_quantize(x, TH_X, SC_X)
        w_q = ternary_quantize(weight, TH_W, SC_W)
        w_rram = w_q + rram_variation
        return jnp.einsum('bsd,od->bso', x_q, w_rram)
    x = L0_attn_hidden_states
    x = x + _L0_attn_ref(_layernorm(x, axis=-1), L0_attn_Wqkv, L0_attn_q_norm_w, L0_attn_k_norm_w, L0_attn_Wo)
    x = x + _L0_ffn_ref(_layernorm(x, axis=-1), L0_ffn_weight, L0_ffn_rram_variation)
    return x

_drawn_inputs = setup_inputs


def setup_inputs(seed=0):
    import zlib

    import numpy as np

    out = dict(_drawn_inputs(seed))
    spreads = {'L0_attn_q_norm_w': (1.0, 0.2), 'L0_attn_k_norm_w': (1.0, 0.2)}
    factors = {}
    for name, (base, spread) in spreads.items():
        noise = np.random.default_rng([zlib.crc32(name.encode()), seed]).standard_normal(out[name].shape)
        drawn = base * np.exp(spread * noise) if base else spread * noise
        out[name] = jnp.asarray(drawn.astype(out[name].dtype))
    for name, factor in factors.items():
        out[name] = (out[name] * factor).astype(out[name].dtype)
    return out
```

```python
from contextlib import ExitStack

import numpy as np

import concourse.bass as bass
from concourse import mybir

F32 = mybir.dt.float32
F32R = mybir.dt.float32r
BF16 = mybir.dt.bfloat16
U32 = mybir.dt.uint32
ALU = mybir.AluOpType
ACT = mybir.ActivationFunctionType
AX_X = mybir.AxisListType.X

P = 128
SEQ, DIM = 2048, 512
HEADS, HEAD_DIM = 16, 32
HALF = HEAD_DIM // 2
WINDOW = 256
TILES = SEQ // P
CHUNKS = DIM // P
GROUP = 512
GT = GROUP // P
GROUPS = SEQ // GROUP
PAIRS = TILES // 2
STEPS = HEADS * PAIRS
STACKED = 3 * HEAD_DIM
MAXROWS = 2
NSTACK = 3
ST_LAG = 9
PV_LAG = 10
NPT = 4
LN_EPS, RMS_EPS, THETA = 1e-5, 1e-6, 10000.0
SCALE = 1.0 / float(np.sqrt(HEAD_DIM))
TH_X, SC_X, TH_W, SC_W = 0.33, 0.5, 0.2, 0.6
LOWEST = -3.0e38


class Steps:

    def __init__(self, sem):
        self.sem = sem

    def done(self, instruction):
        return instruction.then_inc(self.sem, 1)

    def wait(self, engine, i):
        if i >= 0:
            engine.wait_ge(self.sem, i + 1)


class Arrivals:

    def __init__(self, sem, parts=1):
        self.sem, self.parts = sem, parts

    def sent(self, instruction):
        return instruction.then_inc(self.sem, 16)

    def wait(self, engine, use):
        if use >= 0:
            engine.wait_ge(self.sem, 16 * self.parts * (use + 1))


def build(nc, x_d, wqkv_d, qkw_d, wo_d, wf_d, rram_d, cos_d, sin_d, ident_d, out_d):
    ctx = ExitStack()
    with ctx:
        def sb(name, shape, dt=F32):
            return ctx.enter_context(nc.sbuf_tensor(name, shape, dt))

        def steps(name):
            return Steps(ctx.enter_context(nc.semaphore(name)))

        def arrivals(name, parts=1):
            return Arrivals(ctx.enter_context(nc.semaphore(name)), parts)

        qk_scr = nc.dram_tensor("qk_scr", [2, HEADS, 3, HEAD_DIM, SEQ], F32, kind="Internal").ap()
        sum_scr = nc.dram_tensor("sum_scr", [HEADS, SEQ], F32, kind="Internal").ap()
        zero_scr = nc.dram_tensor("zero_scr", [MAXROWS, SEQ], F32, kind="Internal").ap()
        rec_scr = nc.dram_tensor("rec_scr", [HEADS, SEQ], F32, kind="Internal").ap()

        region_w = sb("region_w", [P, 12288], F32R)
        wqkv = region_w[:, :].rearrange("p (s k n) -> p s k n", s=2, k=CHUNKS)
        q_stack = [region_w[:, 4096 * i:4096 * i + SEQ] for i in range(NSTACK)]
        k_stack = [region_w[:, 4096 * i + SEQ:4096 * i + 2 * SEQ] for i in range(NSTACK)]
        o_split = [region_w[:, 4096 * i:4096 * (i + 1)].rearrange("p (s c t) -> p s c t", s=2, c=CHUNKS)
                   for i in range(2)]
        xq_t = [region_w[:, 8192 + 512 * i:8192 + 512 * (i + 1)].rearrange("p (c t) -> p c t", c=CHUNKS)
                for i in range(2)]

        region_t = sb("region_t", [P, 8192], F32R)
        x_t = [region_t[:, 4096 * i:4096 * (i + 1)].rearrange("p (s k t) -> p s k t", s=2, k=CHUNKS)
               for i in range(2)]
        wo = region_t[:, 0:4096].rearrange("p (s k n) -> p s k n", s=2, k=CHUNKS)
        wf = region_t[:, 4096:8192].rearrange("p (s k n) -> p s k n", s=2, k=CHUNKS)

        region_o = sb("region_o", [P, 8192])
        w_raw = region_o[:, 0:6144].rearrange("p (k n) -> p k n", k=CHUNKS)
        rope = region_o[:, 0:2048].rearrange("p (i t) -> p i t", i=4)
        unit = region_o[:, 2048:6144].rearrange("p (i t) -> p i t", i=8)
        square = region_o[:, 6144:7168].rearrange("p (i t) -> p i t", i=2)
        sqsum = region_o[:, 7168:8192].rearrange("p (i t) -> p i t", i=2)
        o_t = region_o[:, :].rearrange("p (c t) -> p c t", c=CHUNKS)

        v = sb("v", [P, TILES, DIM])
        region_m = sb("region_m", [P, 5120])
        x_in = region_m[:, 0:2048].rearrange("p (i n) -> p i n", i=GT)
        x_hat = region_m[:, 2048:3072].rearrange("p (i n) -> p i n", i=2)
        trig = region_m[:, 3072:5120].rearrange("p (i s t) -> p i s t", i=2, s=2)
        prob = region_m[:, 0:3072].rearrange("p (i e t) -> p i e t", i=NPT, e=2)
        o_stage = region_m[:, 3072:4096].rearrange("p (i t) -> p i t", i=2)
        x3 = region_m[:, 0:2048].rearrange("p (i n) -> p i n", i=4)
        x1 = region_m[:, 2048:4096].rearrange("p (i n) -> p i n", i=4)
        y3 = region_m[:, 4096:5120].rearrange("p (i n) -> p i n", i=2)

        normed = sb("normed", [P, 4, GROUP])
        out_stage = normed
        half_h = sb("half_h", [P, 2, GROUP], F32R)
        half_l = sb("half_l", [P, 2, GROUP], F32R)
        stage_w = sb("stage_w", [P, 2, 1024])
        rec_bc = sb("rec_bc", [P, SEQ])
        diag = sb("diag", [P, 2, GROUP])
        ident = sb("ident", [P, P])
        ident_bf = sb("ident_bf", [P, P], BF16)
        ones = sb("ones", [P, P])
        mask = sb("mask", [P, 2, P])
        qkw = sb("qkw", [P, 8])
        ln_bias = sb("ln_bias", [P, 2])
        stats = sb("stats", [P, GT, 6])
        mean_var = sb("mean_var", [P, GT, 2])
        dev = sb("dev", [P, GT])
        rstd = sb("rstd", [P, GT])
        rms_dev = sb("rms_dev", [P, 2, GT])
        rms_rec = sb("rms_rec", [P, 2, GT])
        neg_max = sb("neg_max", [P, 2, TILES])
        max_split = sb("max_split", [P, 2, 2 * PAIRS], F32R)
        max_rows = sb("max_rows", [2 * PAIRS, 2, P], F32R)
        w_fold = region_m[:, 4096:5120].rearrange("p (i n) -> p i n", i=2)
        sums = sb("sums", [P, 64])
        recs = sb("recs", [P, 64])
        below = stage_w[:, 0, 0:DIM].bitcast(BF16).rearrange("p (i n) -> p i n", i=2)
        xq = stage_w[:, 1, 0:DIM].bitcast(BF16).rearrange("p (i n) -> p i n", i=2)

        psum = ctx.enter_context(nc.psum_tensor("psum", [P, 8, 512], F32))
        BANK_XT, BANK_SUMS, BANK_PAIR, BANK_RMS = 0, 1, 2, 6
        BANK_ST, BANK_O = 4, 6
        BANK_WO, BANK_XQ, BANK_FFN = 0, 2, 4

        zero_set, a_zero = steps("zero_set"), arrivals("a_zero")
        const_set, mask_set, ident_cast = steps("const_set"), steps("mask_set"), steps("ident_cast")
        a_const = arrivals("a_const", 2)
        a_w = [arrivals(f"a_w{k}") for k in range(CHUNKS)]
        a_x = arrivals("a_x", GT)
        a_trig = [arrivals(f"a_trig{i}", 2) for i in range(2)]
        a_half = [arrivals(f"a_half{i}", 3) for i in range(2)]
        w_high, w_low = steps("w_high"), steps("w_low")
        bn, aggr, ln_dev, ln_rstd, xhat = (steps(n) for n in ("bn", "aggr", "ln_dev", "ln_rstd", "xhat"))
        xtr, xt_high, xt_low = steps("xtr"), steps("xt_high"), steps("xt_low")
        qk_mm, v_mm, v_out = steps("qk_mm"), steps("v_mm"), steps("v_out")
        roped, squared, rotated, sq_added = steps("roped"), steps("squared"), steps("rotated"), steps("sq_added")
        sq_mm, r_dev, r_rec, diag_s, rms_mm = (steps(n) for n in ("sq_mm", "r_dev", "r_rec", "diag_s", "rms_mm"))
        scaled, q_high, q_low = steps("scaled"), steps("q_high"), steps("q_low")

        a_stack = [arrivals(f"a_stack{i}", 3) for i in range(NSTACK)]
        a_rows = [arrivals(f"a_rows{i}") for i in range(2)]
        a_stage = [arrivals(f"a_stage{i}", 3) for i in range(2)]
        a_sums, a_recs, a_bc = arrivals("a_sums"), arrivals("a_recs"), arrivals("a_bc", 4)
        a_wraw = [arrivals(f"a_wraw{i}") for i in range(2)]
        a_wraw2 = [arrivals(f"a_wraw2{i}", 2) for i in range(2)]
        rows_zero, rows_one, filled, score, merged, maxed = (steps(n) for n in ("rows_zero", "rows_one", "filled", "score", "merged", "maxed"))
        m_high, m_low, m_tr, m_row = steps("m_high"), steps("m_low"), steps("m_tr"), steps("m_row")
        st, expd, selected, pv, staged = (steps(n) for n in ("st", "expd", "selected", "pv", "staged"))
        recd, o_done = steps("recd"), steps("o_done")
        wo_high, wo_low = steps("wo_high"), steps("wo_low")
        w_tern, w_tr, wf_high, wf_low = steps("w_tern"), steps("w_tr"), steps("wf_high"), steps("wf_low")

        a_x3 = [arrivals(f"a_x3{i}") for i in range(4)]
        a_out = [arrivals(f"a_out{i}") for i in range(4)]
        o_high, o_low, wo_mm, x1_s = steps("o_high"), steps("o_low"), steps("wo_mm"), steps("x1_s")
        bn3, aggr3, dev3, rstd3, y_s, below_s, xq_s = (
            steps(n) for n in ("bn3", "aggr3", "dev3", "rstd3", "y_s", "below_s", "xq_s"))
        xq_tr, xq_out, ffn_mm, out_s = steps("xq_tr"), steps("xq_out"), steps("ffn_mm"), steps("out_s")

        def f32(ap):
            return ap.bitcast(F32)

        x_tiles = x_d.rearrange("(t p) n -> t p n", p=P)
        out_tiles = out_d.rearrange("(t p) n -> t p n", p=P)

        def pair_free(engine, n):
            if n < 2:
                return
            g, p = divmod(n - 2, 6)
            if p < 4:
                roped.wait(engine, 4 * (4 * g + p) + 3)
                squared.wait(engine, 8 * g + 2 * p + 1)
            else:
                v_out.wait(engine, 4 * g + 2 * (p - 4) + 1)

        def w_parts(k):
            for half in range(2):
                yield (w_raw[:, k, 0:2 * DIM].rearrange("c (g h x f) -> c x g h f", g=4, x=2, f=HALF)[:, half],
                       lambda s, half=half: wqkv[:, s, k, 0:2 * DIM].rearrange(
                           "c (g x h f) -> c x g h f", g=4, x=2, f=HALF)[:, half])
            yield w_raw[:, k, 2 * DIM:3 * DIM], lambda s: wqkv[:, s, k, 2 * DIM:3 * DIM]

        def head_pair(n):
            return divmod(n, PAIRS)

        M_TR = {4 * c + 5: c for c in range(2 * HEADS)}
        TERN = [24, 32, 40, 48]
        W_TR = {TERN[i // 2] + 2 + 2 * (i % 2): i for i in range(8)}
        STAGED = {4 * c + 4 + PV_LAG: c for c in range(2 * HEADS)}
        RECIP = {32 * c + 32 + 15: c for c in range(CHUNKS)}
        NORM = {32 * c + 32 + 22: c for c in range(CHUNKS)}
        LAST = STEPS + 24
        WO_S = [8, 12, 16, 20]

        block = ctx.enter_context(nc.Block())

        @block.sync
        def _(eng):
            def load_x(g):
                for i in range(GT):
                    a_x.sent(eng.dma_start(x_in[:, i, :], x_tiles[GT * g + i]))

            def load_trig(g):
                cols = slice(GROUP * g, GROUP * (g + 1))
                a_trig[g % 2].sent(eng.dma_start(trig[:, g % 2, 0, :], cos_d[:, cols]))
                a_trig[g % 2].sent(eng.dma_start(trig[:, g % 2, 1, :], sin_d[:, cols]))

            def store_half(g, c):
                n = 8 * g + c
                qk, hg, half = c // 4, (c // 2) % 2, c % 2
                for s in range(3):
                    high = s != (1 if qk else 2)
                    src = half_h if high else half_l
                    if s == 0:
                        q_high.wait(eng, n)
                        q_low.wait(eng, n)
                    dst = qk_scr[qk, 8 * hg:8 * hg + 8, s, HALF * half:HALF * (half + 1),
                                 GROUP * g:GROUP * (g + 1)]
                    a_half[n % 2].sent(eng.dma_start(dst, f32(src[:, n % 2, :])))

            load_x(0)
            for dst, src in ((ident, ident_d), (qkw, qkw_d)):
                a_const.sent(eng.dma_start(dst[:, :], src))
            load_trig(0)
            zero_set.wait(eng, 0)
            a_zero.sent(eng.dma_start(zero_scr, rec_bc[0:MAXROWS, :]))
            xhat.wait(eng, GT - 1)
            load_x(1)
            for g in range(GROUPS):
                if g + 1 < GROUPS:
                    roped.wait(eng, 16 * (g - 1) + 15)
                    load_trig(g + 1)
                if g:
                    for c in range(4, 8):
                        store_half(g - 1, c)
                if g + 2 < GROUPS:
                    xhat.wait(eng, GT * (g + 1) + 3)
                    load_x(g + 2)
                for c in range(4):
                    store_half(g, c)
            for c in range(4, 8):
                store_half(GROUPS - 1, c)

            def load_stack(h):
                if h >= NSTACK:
                    st.wait(eng, 2 * PAIRS * (h - NSTACK + 1) - 1)
                else:
                    rows_zero.wait(eng, 2 * h + 1)
                a_stack[h % NSTACK].sent(eng.dma_start(
                    f32(q_stack[h % NSTACK][STACKED:STACKED + MAXROWS, :]), zero_scr))
                for qk, stack in ((0, q_stack), (1, k_stack)):
                    a_stack[h % NSTACK].sent(eng.dma_start(
                        f32(stack[h % NSTACK][0:STACKED, :]), qk_scr[qk, h].rearrange("s d t -> (s d) t")))

            for i in range(2):
                a_half[i].wait(eng, 4 * GROUPS - 1)
            v_mm.wait(eng, TILES - 1)
            a_zero.wait(eng, 0)
            load_stack(0)
            load_stack(1)
            for s in range(LAST):
                if s == 0:
                    load_stack(2)
                if s in M_TR:
                    c = M_TR[s]
                    h, half = divmod(c, 2)
                    m_row.wait(eng, c)
                    dst = q_stack[h % NSTACK][STACKED:STACKED + MAXROWS, 1024 * half:1024 * (half + 1)]
                    a_rows[c % 2].sent(eng.dma_start(f32(dst), f32(max_rows[:, c % 2, :])))
                h = s // PAIRS + 1
                if s % PAIRS == 1 and NSTACK <= h < HEADS:
                    load_stack(h)
                if s in STAGED:
                    c = STAGED[s]
                    h, half = divmod(c, 2)
                    staged.wait(eng, c)
                    tokens = slice(1024 * half, 1024 * (half + 1))
                    rows = HEAD_DIM * (h % 4)
                    for e in range(2):
                        dst = o_t[rows:rows + HEAD_DIM, h // 4, tokens].rearrange("p (j e t) -> p e j t", e=2, t=P)
                        src = o_stage[64 * e:64 * e + HEAD_DIM, c % 2, :].rearrange("p (j t) -> p j t", t=P)
                        a_stage[c % 2].sent(eng.dma_start(dst[:, e], src))
                    dst = sum_scr[h, tokens].rearrange("(j e t) -> e j t", e=2, t=P)
                    src = o_stage[HEAD_DIM:HEAD_DIM + 65:64, c % 2, :].rearrange("p (j t) -> p j t", t=P)
                    a_stage[c % 2].sent(eng.dma_start(dst, src))
                if s + 1 in RECIP:
                    c = RECIP[s + 1]
                    for i in range(2):
                        a_stage[i].wait(eng, 4 * c + 3)
                    a_sums.sent(eng.dma_start(sums[:, :], sum_scr[4 * c:4 * c + 4, :].rearrange(
                        "h (i t) -> (h i) t", t=64)))
                if s - 2 in RECIP:
                    c = RECIP[s - 2]
                    recd.wait(eng, c)
                    a_recs.sent(eng.dma_start(rec_scr[4 * c:4 * c + 4, :].rearrange("h (i t) -> (h i) t", t=64),
                                              recs[:, :]))
                if s - 4 in RECIP:
                    c = RECIP[s - 4]
                    a_recs.wait(eng, c)
                    if c:
                        o_done.wait(eng, c - 1)
                    for h in range(4):
                        a_bc.sent(eng.dma_start(rec_bc[HEAD_DIM * h:HEAD_DIM * (h + 1), :],
                                                rec_scr[4 * c + h:4 * c + h + 1, :].to_broadcast([HEAD_DIM, SEQ])))
                if s + 6 in WO_S:
                    k = WO_S.index(s + 6)
                    if k >= 2:
                        wo_low.wait(eng, k - 2)
                    a_wraw[k % 2].sent(eng.dma_start(stage_w[:, k % 2, 0:DIM], wo_d[P * k:P * (k + 1), :]))
                if s + 2 in TERN:
                    k = TERN.index(s + 2)
                    if k == 0:
                        wo_low.wait(eng, 3)
                    if k >= 2:
                        w_tern.wait(eng, 4 * (k - 2) + 3)
                    a_wraw2[k % 2].sent(eng.dma_start(stage_w[:, k % 2, 0:DIM], wf_d[P * k:P * (k + 1), :]))
                    a_wraw2[k % 2].sent(eng.dma_start(stage_w[:, k % 2, DIM:2 * DIM], rram_d[P * k:P * (k + 1), :]))

            expd.wait(eng, 2 * STEPS - 1)
            selected.wait(eng, 2 * STEPS - HEADS - 1)
            pv.wait(eng, STEPS - 1)
            def load_x3(t):
                if t >= 4:
                    x1_s.wait(eng, t - 4)
                a_x3[t % 4].sent(eng.dma_start(x3[:, t % 4, :], x_tiles[t]))
            for t in range(4):
                load_x3(t)
            for t in range(TILES):
                if t + 4 < TILES:
                    load_x3(t + 4)
                if t >= 3:
                    out_s.wait(eng, t - 3)
                    a_out[(t - 3) % 4].sent(eng.dma_start(out_tiles[t - 3], out_stage[:, (t - 3) % 4, :]))
            for t in range(TILES - 3, TILES):
                out_s.wait(eng, t)
                a_out[t % 4].sent(eng.dma_start(out_tiles[t], out_stage[:, t % 4, :]))
            for i in range(4):
                a_out[i].wait(eng, TILES // 4 - 1)

        @block.tensor
        def _(eng):
            SPLIT = ((0, 0), (0, 1), (1, 0))

            def transpose_x(t):
                xhat.wait(eng, t)
                xt_high.wait(eng, t - 1)
                xt_low.wait(eng, t - 1)
                for k in range(CHUNKS):
                    last = nc.tensor.transpose(psum[:, BANK_XT, P * k:P * (k + 1)],
                                               x_hat[:, t % 2, P * k:P * (k + 1)], ident[:, :])
                xtr.done(last)

            def project_qk(g, p):
                n = 6 * g + p
                pair_free(eng, n)
                for half in range(2):
                    out = psum[:, BANK_PAIR + 2 * (n % 2) + half, :]
                    i = 0
                    for k in range(CHUNKS):
                        for a, b in SPLIT:
                            w = wqkv[:, a, k, 256 * p + P * half:256 * p + P * (half + 1)]
                            last = nc.tensor.matmul(out, w, x_t[g % 2][:, b, k, :],
                                                    start=(i == 0), stop=(i == 11))
                            i += 1
                    qk_mm.done(last)

            def project_v(g, p):
                n = 6 * g + 4 + p
                pair_free(eng, n)
                for e in range(2):
                    i = 2 * p + e
                    out = psum[:, BANK_PAIR + 2 * (n % 2) + e, :]
                    j = 0
                    for k in range(CHUNKS):
                        for a, b in SPLIT:
                            last = nc.tensor.matmul(out, x_t[g % 2][:, b, k, P * i:P * (i + 1)],
                                                    wqkv[:, a, k, 2 * DIM:3 * DIM], start=(j == 0), stop=(j == 11))
                            j += 1
                    v_mm.done(last)

            def sum_squares(g, s):
                sq_added.wait(eng, 6 * g + 3 * s + 2)
                r_dev.wait(eng, 2 * g + s - 1)
                for i in range(GT):
                    last = nc.tensor.matmul(psum[:, BANK_SUMS, i:i + 1], sqsum[:, s, P * i:P * (i + 1)],
                                            ones[:, 0:1], start=True, stop=True)
                sq_mm.done(last)

            def spread_rms(g, s):
                diag_s.wait(eng, GT * (2 * g + s) + GT - 1)
                if g:
                    scaled.wait(eng, 8 * (g - 1) + 4 * s + 3)
                rms_mm.done(nc.tensor.matmul(psum[:, BANK_RMS + s, :], ones[:, :], diag[:, s, :],
                                             start=True, stop=True))

            a_const.wait(eng, 0)
            const_set.wait(eng, 3)
            for t in range(GT):
                transpose_x(t)
            w_high.wait(eng, 3 * CHUNKS - 1)
            w_low.wait(eng, 3 * CHUNKS - 1)
            for g in range(GROUPS):
                xt_high.wait(eng, GT * g + 3)
                xt_low.wait(eng, GT * g + 3)
                for p in range(4):
                    project_qk(g, p)
                    if p == 0 and g:
                        spread_rms(g - 1, 1)
                    if g + 1 < GROUPS:
                        transpose_x(GT * (g + 1) + p)
                sum_squares(g, 0)
                project_v(g, 0)
                spread_rms(g, 0)
                if g == GROUPS - 1:
                    sum_squares(g, 1)
                project_v(g, 1)
                if g < GROUPS - 1:
                    sum_squares(g, 1)
            spread_rms(GROUPS - 1, 1)

            def scores(n):
                h, j = head_pair(n)
                if j == 0:
                    a_stack[h % NSTACK].wait(eng, h // NSTACK)
                    filled.wait(eng, h)
                    rows_one.wait(eng, min(h, NSTACK - 1))
                if n >= 2:
                    maxed.wait(eng, n - 2)
                elif n == 0:
                    r_dev.wait(eng, 2 * GROUPS - 1)
                    xt_low.wait(eng, TILES - 1)
                else:
                    v_out.wait(eng, TILES - 1)
                qs, ks = q_stack[h % NSTACK], k_stack[h % NSTACK]
                for e in range(2):
                    qt = 2 * j + e
                    k0 = max(0, qt - 2)
                    last = nc.tensor.matmul(psum[:, 2 * (n % 2) + e, P * (k0 - qt + 2):3 * P],
                                            qs[:, P * qt:P * (qt + 1)],
                                            ks[:, P * k0:P * (qt + 1)], start=True, stop=True)
                score.done(last)

            def maxima_to_rows(c, s):
                m_low.wait(eng, c)
                m_tr.done(nc.tensor.transpose(psum[0:2 * PAIRS, 2 * (s % 2), 3 * P:4 * P],
                                              f32(max_split[:, c % 2, :]), ident[:, :]))

            def transpose_w(i):
                k, d0 = divmod(i, 2)
                w_tern.wait(eng, 4 * k + 3)
                return k, 2 * d0

            def scores_t(n):
                h, j = head_pair(n)
                c = 2 * h + min(2 * j + 3, TILES - 1) // PAIRS
                a_rows[c % 2].wait(eng, c // 2)
                qs, ks = q_stack[h % NSTACK], k_stack[h % NSTACK]
                for e in range(2):
                    kt = 2 * j + e
                    expd.wait(eng, 2 * (n - 1) + e)
                    q1 = min(TILES, kt + 3)
                    last = nc.tensor.matmul(psum[:, BANK_ST + e, 0:P * (q1 - kt)],
                                            ks[:, P * kt:P * (kt + 1)],
                                            qs[:, P * kt:P * q1], start=True, stop=True)
                    st.done(last)

            def times_v(n):
                h, j = head_pair(n)
                c = n // 4
                selected.wait(eng, (2 * PAIRS - 1) * h + min(2 * j + 1, 2 * PAIRS - 2))
                if n % 4 == 0:
                    staged.wait(eng, c - 2)
                    if n == 0:
                        scaled.wait(eng, 8 * GROUPS - 1)
                cols = slice(P * (n % 4), P * (n % 4 + 1))
                for b in range(3):
                    for e in range(2):
                        qt = 2 * j + e
                        kt = qt - 2 + b
                        if kt < 0:
                            continue
                        probs = prob[:, (n - j + kt // 2) % NPT, kt % 2, P * (qt - kt):P * (qt - kt + 1)]
                        for r, w in ((2 * e, v[:, kt, HEAD_DIM * h:HEAD_DIM * (h + 1)]),
                                     (2 * e + 1, ones[:, 0:HEAD_DIM])):
                            last = nc.tensor.matmul(psum[32 * r:32 * r + 32, BANK_O + c % 2, cols], w, probs,
                                                    start=(kt == max(0, qt - 2)), stop=(kt == qt),
                                                    tile_position=(0, 32 * r))
                pv.done(last)

            for s in range(STEPS + PV_LAG):
                if 0 <= s - ST_LAG < STEPS:
                    scores_t(s - ST_LAG)
                if s < STEPS:
                    scores(s)
                else:
                    if s - 2 < STEPS:
                        maxed.wait(eng, s - 2)
                if s in M_TR:
                    maxima_to_rows(M_TR[s], s)
                if s in W_TR:
                    k, d0 = transpose_w(W_TR[s])
                    for e in range(2):
                        last = nc.tensor.transpose(psum[:, 2 * (s % 2) + e, 3 * P:4 * P],
                                                   w_fold[:, k % 2, P * (d0 + e):P * (d0 + e + 1)], ident[:, :])
                    w_tr.done(last)
                if 0 <= s - PV_LAG < STEPS:
                    times_v(s - PV_LAG)

            def project_o(t):
                g, i = divmod(t, GT)
                o_high.wait(eng, CHUNKS * g + CHUNKS - 1)
                o_low.wait(eng, CHUNKS * g + CHUNKS - 1)
                if t == 0:
                    wo_high.wait(eng, CHUNKS - 1)
                    wo_low.wait(eng, CHUNKS - 1)
                    m_row.wait(eng, 2 * HEADS - 1)
                if t >= 2:
                    x1_s.wait(eng, t - 2)
                else:
                    maxed.wait(eng, STEPS - 2 + t)
                j = 0
                for c in range(CHUNKS):
                    for a, b in SPLIT:
                        last = nc.tensor.matmul(psum[:, BANK_WO + t % 2, :],
                                                o_split[g % 2][:, a, c, P * i:P * (i + 1)], wo[:, b, c, :],
                                                start=(j == 0), stop=(j == 11))
                        j += 1
                wo_mm.done(last)

            def transpose_xq(t):
                xq_s.wait(eng, t)
                xq_out.wait(eng, t - 2)
                for c in range(CHUNKS):
                    last = nc.tensor.transpose(psum[:, BANK_XQ + t % 2, 0:DIM // 2].bitcast(BF16)[:, P * c:P * (c + 1)],
                                               xq[:, t % 2, P * c:P * (c + 1)], ident_bf[:, :])
                xq_tr.done(last)

            def ffn(t):
                xq_out.wait(eng, t)
                if t == 0:
                    wf_low.wait(eng, 15)
                if t >= 2:
                    out_s.wait(eng, t - 2)
                else:
                    expd.wait(eng, 2 * STEPS - 1)
                j = 0
                for c in range(CHUNKS):
                    for a in range(2):
                        last = nc.tensor.matmul(psum[:, BANK_FFN + t % 2, :], xq_t[t % 2][:, c, :], wf[:, a, c, :],
                                                start=(j == 0), stop=(j == 7))
                        j += 1
                ffn_mm.done(last)

            for t in range(TILES + 3):
                if t < TILES:
                    project_o(t)
                if 0 <= t - 2 < TILES:
                    transpose_xq(t - 2)
                if 0 <= t - 3 < TILES:
                    ffn(t - 3)

        @block.scalar
        def _(eng):
            for k in range(CHUNKS):
                a_w[k].sent(eng.dma_start(w_raw[:, k, :], wqkv_d[P * k:P * (k + 1), :]))
            const_set.wait(eng, 3)

            def ln_sqrt(g):
                aggr.wait(eng, GT * g + 3)
                ln_rstd.wait(eng, g - 1)
                ln_dev.done(nc.scalar.activation(dev[:, :], mean_var[:, :, 1], ACT.Sqrt, bias=ln_bias[:, 0:1]))

            def high_x(t):
                xtr.wait(eng, t)
                g, i = divmod(t, GT)
                if g >= 2:
                    v_mm.wait(eng, GT * (g - 2) + 3)
                xt_high.done(nc.scalar.copy(x_t[g % 2][:, 0, :, P * i:P * (i + 1)],
                                            psum[:, BANK_XT, :].rearrange("p (k t) -> p k t", k=CHUNKS)))

            def squares(g, p):
                for half in range(2):
                    c = 2 * p + half
                    qk_mm.wait(eng, 8 * g + c)
                    m = 4 * g + p - 1
                    if m >= 0:
                        sq_added.wait(eng, 3 * (m // 2) + (0 if m % 2 == 0 else 2))
                    if m < 0 and half == 0:
                        w_low.wait(eng, 3 * CHUNKS - 1)
                    squared.done(nc.scalar.activation(square[:, half, :],
                                                      psum[:, BANK_PAIR + 2 * ((6 * g + p) % 2) + half, :],
                                                      ACT.Square))

            def rms_sqrt(g, s):
                m = 2 * g + s
                sq_mm.wait(eng, m)
                if g:
                    r_rec.wait(eng, m - 2)
                r_dev.done(nc.scalar.activation(rms_dev[:, s, :], psum[:, BANK_SUMS, 0:GT], ACT.Sqrt,
                                                bias=ln_bias[:, 1:2], scale=1.0 / DIM))

            def evacuate_v(g, p):
                for e in range(2):
                    t = GT * g + 2 * p + e
                    v_mm.wait(eng, t)
                    v_out.done(nc.scalar.copy(v[:, t, :], psum[:, BANK_PAIR + 2 * ((6 * g + 4 + p) % 2) + e, :]))

            def high_qk(g, s):
                for c in range(4 * s, 4 * s + 4):
                    n = 8 * g + c
                    scaled.wait(eng, n)
                    a_half[n % 2].wait(eng, n // 2 - 1)
                    q_high.done(nc.scalar.copy(half_h[:, n % 2, :], normed[:, n % 4, :]))

            ln_sqrt(0)
            for t in range(2):
                high_x(t)
            for k in range(CHUNKS):
                a_w[k].wait(eng, 0)
                for raw, kept in w_parts(k):
                    w_high.done(nc.scalar.copy(kept(0), raw))
                if k < 2:
                    high_x(2 + k)
            for g in range(GROUPS):
                if g + 1 < GROUPS:
                    ln_sqrt(g + 1)
                for p in range(4):
                    squares(g, p)
                    if g + 1 < GROUPS:
                        high_x(GT * (g + 1) + p)
                    if p == 1 and g:
                        high_qk(g - 1, 1)
                rms_sqrt(g, 0)
                evacuate_v(g, 0)
                if g == GROUPS - 1:
                    rms_sqrt(g, 1)
                high_qk(g, 0)
                evacuate_v(g, 1)
                if g < GROUPS - 1:
                    rms_sqrt(g, 1)
            high_qk(GROUPS - 1, 1)

            def exponentials(n):
                h, j = head_pair(n)
                pv.wait(eng, n - 3)
                if n == 0:
                    xtr.wait(eng, TILES - 1)
                    roped.wait(eng, 16 * GROUPS - 1)
                for e in range(2):
                    st.wait(eng, 2 * n + e)
                    cols = P * min(3, TILES - 2 * j - e)
                    expd.done(nc.scalar.activation(prob[:, n % NPT, e, 0:cols], psum[:, BANK_ST + e, 0:cols],
                                                   ACT.Exp, scale=SCALE))

            def stage(c):
                pv.wait(eng, 4 * c + 3)
                if c >= 2:
                    a_stage[c % 2].wait(eng, c // 2 - 1)
                staged.done(nc.scalar.copy(o_stage[:, c % 2, :], psum[:, BANK_O + c % 2, :]))

            for s in range(STEPS + PV_LAG + 2):
                if 0 <= s - ST_LAG < STEPS:
                    exponentials(s - ST_LAG)
                if s in STAGED:
                    stage(STAGED[s])
                if s in WO_S:
                    k = WO_S.index(s)
                    a_wraw[k % 2].wait(eng, k // 2)
                    wo_high.done(nc.scalar.copy(wo[:, 0, k, :], stage_w[:, k % 2, 0:DIM]))

            def high_o(g):
                for c in range(CHUNKS):
                    o_done.wait(eng, c)
                    if g == 0 and c == 0:
                        st.wait(eng, 2 * STEPS - 1)
                    if g >= 2:
                        wo_mm.wait(eng, GT * (g - 2) + 3)
                    o_high.done(nc.scalar.copy(o_split[g % 2][:, 0, c, :], o_t[:, c, GROUP * g:GROUP * (g + 1)]))

            high_o(0)
            for t in range(TILES + 2):
                if t < TILES:
                    if t % GT == 1 and t // GT + 1 < GROUPS:
                        high_o(t // GT + 1)
                    aggr3.wait(eng, t)
                    rstd3.wait(eng, t - 4)
                    dev3.done(nc.scalar.activation(dev[:, t % 4:t % 4 + 1], mean_var[:, t % 4, 1:2], ACT.Sqrt,
                                                   bias=ln_bias[:, 0:1]))
                if 0 <= t - 2 < TILES:
                    u = t - 2
                    xq_tr.wait(eng, u)
                    ffn_mm.wait(eng, u - 2)
                    xq_out.done(nc.scalar.copy(
                        xq_t[u % 2][:, :, :],
                        psum[:, BANK_XQ + u % 2, 0:DIM // 2].bitcast(BF16).rearrange("p (c t) -> p c t", c=CHUNKS)))

        @block.gpsimd
        def _(eng):
            const_set.done(nc.gpsimd.memset(ones[:, :], 1.0))
            const_set.done(nc.gpsimd.memset(ln_bias[:, 0:1], LN_EPS))
            const_set.done(nc.gpsimd.memset(ln_bias[:, 1:2], RMS_EPS))
            const_set.done(nc.gpsimd.memset(mask[:, :, :], 1.0))
            zero_set.done(nc.gpsimd.memset(rec_bc[:, :], 0.0))
            const_set.wait(eng, 3)
            mask_set.done(nc.gpsimd.affine_select(out=mask[:, :, :], in_=mask[:, :, :], compare_op=ALU.is_ge,
                                                  fill=0.0, base=0, pattern=[[0, 2], [-1, P]],
                                                  channel_multiplier=1))

            def rotate(g, p):
                m = 4 * g + p
                u = 4 * (p // 2) + 2 * (p % 2)
                if g:
                    scaled.wait(eng, 8 * (g - 1) + 2 * p + 1)
                roped.wait(eng, 4 * m + 1)
                rotated.done(nc.gpsimd.tensor_tensor(unit[:, u, :], rope[:, 0, :], rope[:, 1, :], ALU.subtract))
                roped.wait(eng, 4 * m + 3)
                rotated.done(nc.gpsimd.tensor_tensor(unit[:, u + 1, :], rope[:, 2, :], rope[:, 3, :], ALU.add))

            def add_squares(g, p):
                s = p // 2
                squared.wait(eng, 8 * g + 2 * p + 1)
                if p % 2 == 0:
                    if g:
                        sq_mm.wait(eng, 2 * (g - 1) + s)
                    sq_added.done(nc.gpsimd.tensor_tensor(sqsum[:, s, :], square[:, 0, :], square[:, 1, :], ALU.add))
                else:
                    for half in range(2):
                        n = 6 * g + 3 * s + 1 + half
                        sq_added.wait(eng, n - 1)
                        sq_added.done(nc.gpsimd.tensor_tensor(sqsum[:, s, :], sqsum[:, s, :], square[:, half, :],
                                                              ALU.add))

            def low_qk(g, s):
                for c in range(4 * s, 4 * s + 4):
                    n = 8 * g + c
                    q_high.wait(eng, n)
                    a_half[n % 2].wait(eng, n // 2 - 1)
                    q_low.done(nc.gpsimd.tensor_tensor(half_l[:, n % 2, :], normed[:, n % 4, :],
                                                       f32(half_h[:, n % 2, :]), ALU.subtract))

            for g in range(GROUPS):
                for p in range(4):
                    rotate(g, p)
                    add_squares(g, p)
                    if p == 1 and g:
                        low_qk(g - 1, 1)
                low_qk(g, 0)
            low_qk(GROUPS - 1, 1)

            for n in range(STEPS):
                h, j = head_pair(n)
                expd.wait(eng, 2 * n + 1)
                near = prob[:, n % NPT, :, 0:P]
                selected.done(nc.gpsimd.affine_select(out=near, in_=near, compare_op=ALU.is_ge, fill=0.0, base=0,
                                                      pattern=[[0, 2], [1, P]], channel_multiplier=-1))
                if j < PAIRS - 1:
                    far = prob[:, n % NPT, :, 2 * P:3 * P]
                    selected.done(nc.gpsimd.affine_select(out=far, in_=far, compare_op=ALU.is_ge, fill=0.0,
                                                          base=WINDOW - 1 - 2 * P, pattern=[[0, 2], [-1, P]],
                                                          channel_multiplier=1))

            for g in range(GROUPS):
                for c in range(CHUNKS):
                    o_high.wait(eng, CHUNKS * g + c)
                    o_low.done(nc.gpsimd.tensor_tensor(o_split[g % 2][:, 1, c, :], o_t[:, c, GROUP * g:GROUP * (g + 1)],
                                                       f32(o_split[g % 2][:, 0, c, :]), ALU.subtract))

        @block.vector
        def _(eng):
            vec = nc.vector

            def ln_stats(g):
                for i in range(GT):
                    a_x.wait(eng, g)
                    xhat.wait(eng, GT * (g - 1) + i)
                    bn.done(vec.bn_stats(stats[:, i, :], x_in[:, i, :]))
                for i in range(GT):
                    bn.wait(eng, GT * g + i)
                    aggr.done(vec.bn_aggr(mean_var[:, i, :], stats[:, i, :]))

            def ln_recip(g):
                ln_dev.wait(eng, g)
                ln_rstd.done(vec.reciprocal(rstd[:, :], dev[:, :]))

            def normalise(t):
                g, i = divmod(t, GT)
                ln_rstd.wait(eng, g)
                xtr.wait(eng, t - 2)
                xhat.done(vec.tensor_scalar(x_hat[:, t % 2, :], x_in[:, i, :], mean_var[:, i, 0:1],
                                            rstd[:, i:i + 1], ALU.subtract, ALU.mult))

            def low_x(t):
                g, i = divmod(t, GT)
                xt_high.wait(eng, t)
                xt_low.done(vec.tensor_tensor(x_t[g % 2][:, 1, :, P * i:P * (i + 1)],
                                              psum[:, BANK_XT, :].rearrange("p (k t) -> p k t", k=CHUNKS),
                                              f32(x_t[g % 2][:, 0, :, P * i:P * (i + 1)]), ALU.subtract))

            def rope_products(g, p):
                m = 4 * g + p
                banks = BANK_PAIR + 2 * ((6 * g + p) % 2)
                squared.wait(eng, 8 * g + 2 * p + 1)
                a_trig[g % 2].wait(eng, g // 2)
                for i, (half, s) in enumerate(((0, 0), (1, 1), (1, 0), (0, 1))):
                    if m:
                        rotated.wait(eng, 2 * (m - 1) + i // 2)
                    roped.done(vec.scalar_tensor_tensor(rope[:, i, :], psum[:, banks + half, :],
                                                        qkw[:, 2 * p + half:2 * p + half + 1],
                                                        trig[:, g % 2, s, :], ALU.mult, ALU.mult))

            def rms_recip(g, s):
                m = 2 * g + s
                r_dev.wait(eng, m)
                r_rec.done(vec.reciprocal(rms_rec[:, s, :], rms_dev[:, s, :]))
                r_rec.wait(eng, m)
                if g:
                    rms_mm.wait(eng, m - 2)
                for i in range(GT):
                    diag_s.done(vec.tensor_scalar(diag[:, s, P * i:P * (i + 1)], ident[:, :],
                                                  rms_rec[:, s, i:i + 1], None, ALU.mult))

            def scale_qk(g, s):
                rms_mm.wait(eng, 2 * g + s)
                for c in range(4 * s, 4 * s + 4):
                    n = 8 * g + c
                    rotated.wait(eng, n)
                    q_low.wait(eng, n - 4)
                    scaled.done(vec.tensor_tensor(normed[:, n % 4, :], unit[:, c, :], psum[:, BANK_RMS + s, :],
                                                  ALU.mult))

            def low_w(k):
                for i, (raw, kept) in enumerate(w_parts(k)):
                    w_high.wait(eng, 3 * k + i)
                    w_low.done(vec.tensor_tensor(kept(1), raw, f32(kept(0)), ALU.subtract))

            a_const.wait(eng, 0)
            ident_cast.done(vec.tensor_copy(ident_bf[:, :], ident[:, :]))
            ln_stats(0)
            ln_recip(0)
            normalise(0)
            normalise(1)
            low_x(0)
            normalise(2)
            low_x(1)
            normalise(3)
            low_w(0)
            low_x(2)
            low_w(1)
            low_x(3)
            low_w(2)
            low_w(3)
            for g in range(GROUPS):
                more = g + 1 < GROUPS
                t = GT * (g + 1)
                if more:
                    ln_stats(g + 1)
                    ln_recip(g + 1)
                    normalise(t)
                    normalise(t + 1)
                for p in range(4):
                    rope_products(g, p)
                    if more:
                        low_x(t + p)
                        if p < 2:
                            normalise(t + 2 + p)
                    if p == 0 and g:
                        scale_qk(g - 1, 1)
                rms_recip(g, 0)
                if g == GROUPS - 1:
                    rms_recip(g, 1)
                scale_qk(g, 0)
                if g < GROUPS - 1:
                    rms_recip(g, 1)
            scale_qk(GROUPS - 1, 1)

            v_mm.wait(eng, TILES - 1)
            for i in range(NSTACK):
                rows_zero.done(vec.memset(f32(q_stack[i][STACKED:P, :]), 0.0))
                rows_zero.done(vec.memset(f32(k_stack[i][STACKED:P, :]), 0.0))
                rows_zero.wait(eng, 2 * i + 1)
                rows_one.done(vec.memset(f32(k_stack[i][STACKED:STACKED + MAXROWS, :]), 1.0))

            def fill(h):
                if h == 0:
                    r_dev.wait(eng, 2 * GROUPS - 1)
                else:
                    maxed.wait(eng, PAIRS * h - 2)
                filled.done(vec.memset(psum[:, 0:2, 0:P], LOWEST))

            def merge(n):
                score.wait(eng, n)
                if n in M_TR:
                    m_tr.wait(eng, M_TR[n])
                if n in W_TR:
                    w_tr.wait(eng, W_TR[n])
                merged.done(vec.copy_predicated(psum[:, 2 * (n % 2):2 * (n % 2) + 2, 0:P], mask[:, :, :].bitcast(U32),
                                                psum[:, 2 * (n % 2):2 * (n % 2) + 2, 2 * P:3 * P]))

            def maximum(n):
                h, j = head_pair(n)
                slot = 2 * (n % 2)
                merged.wait(eng, n)
                if h >= 2:
                    m_low.wait(eng, 2 * (h - 2) + j // 4)
                if j == 0:
                    vec.tensor_reduce(neg_max[:, h % 2, 0:1], psum[:, slot, 0:P], axis=AX_X, op=ALU.max, negate=True)
                    maxed.done(vec.tensor_reduce(neg_max[:, h % 2, 1:2], psum[:, slot + 1, 0:2 * P], axis=AX_X,
                                                 op=ALU.max, negate=True))
                else:
                    maxed.done(vec.tensor_reduce(neg_max[:, h % 2, 2 * j:2 * j + 2], psum[:, slot:slot + 2, 0:2 * P],
                                                 axis=AX_X, op=ALU.max, negate=True))

            def split_maxima(c):
                h, half = divmod(c, 2)
                maxed.wait(eng, 4 * c + 3)
                if c >= 2:
                    m_tr.wait(eng, c - 2)
                cols = neg_max[:, h % 2, PAIRS * half:PAIRS * (half + 1)]
                m_high.done(vec.tensor_copy(max_split[:, c % 2, 0:PAIRS], cols))
                m_high.wait(eng, c)
                m_low.done(vec.tensor_tensor(max_split[:, c % 2, PAIRS:2 * PAIRS], cols,
                                             f32(max_split[:, c % 2, 0:PAIRS]), ALU.subtract))

            def evacuate_rows(c, s):
                m_tr.wait(eng, c)
                if c >= 2:
                    a_rows[c % 2].wait(eng, c // 2 - 1)
                m_row.done(vec.tensor_copy(max_rows[:, c % 2, :], psum[0:2 * PAIRS, 2 * (s % 2), 3 * P:4 * P]))

            def ternary_w(k):
                a_wraw2[k % 2].wait(eng, k // 2)
                if k >= 2:
                    w_tr.wait(eng, 2 * (k - 2) + 1)
                w, var, fold = stage_w[:, k % 2, 0:DIM], stage_w[:, k % 2, DIM:2 * DIM], w_fold[:, k % 2, :]
                w_tern.done(vec.tensor_scalar(fold, w, TH_W, SC_W, ALU.is_gt, ALU.mult))
                w_tern.wait(eng, 4 * k)
                w_tern.done(vec.tensor_scalar(w, w, -TH_W, SC_W, ALU.is_lt, ALU.mult))
                w_tern.wait(eng, 4 * k + 1)
                w_tern.done(vec.tensor_tensor(fold, fold, w, ALU.subtract))
                w_tern.wait(eng, 4 * k + 2)
                w_tern.done(vec.tensor_tensor(fold, fold, var, ALU.add))

            def split_wf(i, s):
                k, d0 = i // 2, 2 * (i % 2)
                w_tr.wait(eng, i)
                for e in range(2):
                    src = psum[:, 2 * (s % 2) + e, 3 * P:4 * P]
                    high = wf[:, 0, d0 + e, P * k:P * (k + 1)]
                    wf_high.done(vec.tensor_scalar(high, src, SC_X, None, ALU.mult))
                    wf_high.wait(eng, 2 * i + e)
                    wf_low.done(vec.scalar_tensor_tensor(wf[:, 1, d0 + e, P * k:P * (k + 1)], src, SC_X, f32(high),
                                                         ALU.mult, ALU.subtract))

            def recip_sums(c):
                a_sums.wait(eng, c)
                if c:
                    a_recs.wait(eng, c - 1)
                recd.done(vec.reciprocal(recs[:, :], sums[:, :]))

            def divide(c):
                a_bc.wait(eng, c)
                o_done.done(vec.tensor_tensor(o_t[:, c, :], o_t[:, c, :], rec_bc[:, :], ALU.mult))

            mask_set.wait(eng, 0)
            fill(0)
            for s in range(LAST):
                if s < STEPS:
                    merge(s)
                if s in M_TR:
                    evacuate_rows(M_TR[s], s)
                if s in W_TR:
                    split_wf(W_TR[s], s)
                if s < STEPS:
                    maximum(s)
                    if s % PAIRS == PAIRS - 2 and s // PAIRS + 1 < HEADS:
                        fill(s // PAIRS + 1)
                    if s % 4 == 3:
                        split_maxima(s // 4)
                if s in WO_S:
                    k = WO_S.index(s)
                    wo_high.wait(eng, k)
                    wo_low.done(vec.tensor_tensor(wo[:, 1, k, :], stage_w[:, k % 2, 0:DIM], f32(wo[:, 0, k, :]),
                                                  ALU.subtract))
                if s in TERN:
                    ternary_w(TERN.index(s))
                if s in RECIP:
                    recip_sums(RECIP[s])
                if s in NORM:
                    divide(NORM[s])

            def residual(t):
                wo_mm.wait(eng, t)
                a_x3[t % 4].wait(eng, t // 4)
                if t >= 4:
                    out_s.wait(eng, t - 4)
                x1_s.done(vec.tensor_tensor(x1[:, t % 4, :], psum[:, BANK_WO + t % 2, :], x3[:, t % 4, :], ALU.add))
                x1_s.wait(eng, t)
                bn3.done(vec.bn_stats(stats[:, t % 4, :], x1[:, t % 4, :]))
                bn3.wait(eng, t)
                y_s.wait(eng, t - 4)
                aggr3.done(vec.bn_aggr(mean_var[:, t % 4, :], stats[:, t % 4, :]))

            def quantise(t):
                dev3.wait(eng, t)
                y_s.wait(eng, t - 4)
                rstd3.done(vec.reciprocal(rstd[:, t % 4:t % 4 + 1], dev[:, t % 4:t % 4 + 1]))
                rstd3.wait(eng, t)
                y = y3[:, t % 2, :]
                y_s.done(vec.tensor_scalar(y, x1[:, t % 4, :], mean_var[:, t % 4, 0:1], rstd[:, t % 4:t % 4 + 1],
                                           ALU.subtract, ALU.mult))
                y_s.wait(eng, t)
                below_s.done(vec.tensor_scalar(below[:, t % 2, :], y, -TH_X, None, ALU.is_lt))
                below_s.wait(eng, t)
                xq_tr.wait(eng, t - 2)
                xq_s.done(vec.scalar_tensor_tensor(xq[:, t % 2, :], y, TH_X, below[:, t % 2, :], ALU.is_gt,
                                                   ALU.subtract))

            def result(t):
                ffn_mm.wait(eng, t)
                if t >= 4:
                    a_out[t % 4].wait(eng, t // 4 - 1)
                out_s.done(vec.tensor_tensor(out_stage[:, t % 4, :], psum[:, BANK_FFN + t % 2, :], x1[:, t % 4, :],
                                             ALU.add))

            for t in range(TILES + 3):
                if t < TILES:
                    residual(t)
                if 0 <= t - 1 < TILES:
                    quantise(t - 1)
                if 0 <= t - 3 < TILES:
                    result(t - 3)


def kernel(L0_attn_hidden_states, L0_attn_Wqkv, L0_attn_q_norm_w, L0_attn_k_norm_w, L0_attn_Wo, L0_ffn_weight,
           L0_ffn_rram_variation):
    import concourse.bacc as bacc
    from concourse.bass_utils import run_bass_kernel_spmd

    f4 = np.float32
    inv_freq = (f4(1.0) / np.power(f4(THETA), np.arange(0, HEAD_DIM, 2, dtype=f4) / f4(HEAD_DIM))).astype(f4)
    angle = (np.arange(SEQ, dtype=f4)[None, :] * inv_freq[:, None]).astype(f4).astype(np.float64)
    cos = np.tile(np.cos(angle).astype(f4), (P // HALF, 1))
    sin = np.tile(np.sin(angle).astype(f4), (P // HALF, 1))

    def by_chunk(w):
        return np.asarray(w).reshape(2, 8, 2, HALF).transpose(1, 3, 0, 2).reshape(P, CHUNKS)

    arrays = {
        "x": np.ascontiguousarray(np.asarray(L0_attn_hidden_states).reshape(SEQ, DIM)),
        "wqkv": np.ascontiguousarray(L0_attn_Wqkv),
        "qkw": np.ascontiguousarray(np.concatenate([by_chunk(L0_attn_q_norm_w), by_chunk(L0_attn_k_norm_w)], 1)),
        "wo": np.ascontiguousarray(L0_attn_Wo),
        "wf": np.ascontiguousarray(L0_ffn_weight),
        "rram": np.ascontiguousarray(L0_ffn_rram_variation),
        "cos": cos, "sin": sin, "ident": np.eye(P, dtype=f4),
    }
    nc = bacc.Bacc("TRN2", target_bir_lowering=False, num_devices=1)
    args = [nc.dram_tensor(f"in_{n}", a.shape, mybir.dt.from_np(a.dtype), kind="ExternalInput").ap()
            for n, a in arrays.items()]
    out = nc.dram_tensor("out", (SEQ, DIM), F32, kind="ExternalOutput").ap()
    build(nc, *args, out)
    result = run_bass_kernel_spmd(nc, [{f"in_{n}": a for n, a in arrays.items()}], core_ids=[0])
    return result.results[0]["out"].reshape(1, SEQ, DIM)
```

```python
from contextlib import ExitStack

import numpy as np

import concourse.bass as bass
from concourse import mybir

F32 = mybir.dt.float32
F32R = mybir.dt.float32r
BF16 = mybir.dt.bfloat16
U32 = mybir.dt.uint32
ALU = mybir.AluOpType
ACT = mybir.ActivationFunctionType
AX_X = mybir.AxisListType.X

P = 128
SEQ, DIM = 2048, 512
HEADS, HEAD_DIM = 16, 32
HALF = HEAD_DIM // 2
WINDOW = 256
TILES = SEQ // P
CHUNKS = DIM // P
GROUP = 512
GT = GROUP // P
GROUPS = SEQ // GROUP
PAIRS = TILES // 2
STEPS = HEADS * PAIRS
STACKED = 3 * HEAD_DIM
MAXROWS = 2
NSTACK = 3
ST_LAG = 10
PV_LAG = 11
NPT = 4
LN_EPS, RMS_EPS, THETA = 1e-5, 1e-6, 10000.0
SCALE = 1.0 / float(np.sqrt(HEAD_DIM))
TH_X, SC_X, TH_W, SC_W = 0.33, 0.5, 0.2, 0.6
LOWEST = -3.0e38


class Steps:

    def __init__(self, sem):
        self.sem = sem

    def done(self, instruction):
        return instruction.then_inc(self.sem, 1)

    def wait(self, engine, i):
        if i >= 0:
            engine.wait_ge(self.sem, i + 1)


class Arrivals:

    def __init__(self, sem, parts=1):
        self.sem, self.parts = sem, parts

    def sent(self, instruction):
        return instruction.then_inc(self.sem, 16)

    def wait(self, engine, use):
        if use >= 0:
            engine.wait_ge(self.sem, 16 * self.parts * (use + 1))


def build(nc, x_d, wqkv_d, qkw_d, wo_d, wf_d, rram_d, cos_d, sin_d, ident_d, out_d):
    ctx = ExitStack()
    with ctx:
        def sb(name, shape, dt=F32):
            return ctx.enter_context(nc.sbuf_tensor(name, shape, dt))

        def steps(name):
            return Steps(ctx.enter_context(nc.semaphore(name)))

        def arrivals(name, parts=1):
            return Arrivals(ctx.enter_context(nc.semaphore(name)), parts)

        qk_scr = nc.dram_tensor("qk_scr", [2, HEADS, 3, HEAD_DIM, SEQ], F32, kind="Internal").ap()
        sum_scr = nc.dram_tensor("sum_scr", [HEADS, SEQ], F32, kind="Internal").ap()
        zero_scr = nc.dram_tensor("zero_scr", [P - STACKED, SEQ], F32, kind="Internal").ap()
        ones_scr = nc.dram_tensor("ones_scr", [P - STACKED, SEQ], F32, kind="Internal").ap()
        rec_scr = nc.dram_tensor("rec_scr", [HEADS, SEQ], F32, kind="Internal").ap()

        region_w = sb("region_w", [P, 12288], F32R)
        wqk = region_w[:, 0:8192].rearrange("p (s k n) -> p s k n", s=2, k=CHUNKS)
        wv = region_w[:, 8192:12288].rearrange("p (s k n) -> p s k n", s=2, k=CHUNKS)
        q_stack = [region_w[:, 4096 * i:4096 * i + SEQ] for i in range(NSTACK)]
        k_stack = [region_w[:, 4096 * i + SEQ:4096 * i + 2 * SEQ] for i in range(NSTACK)]
        o_split = [region_w[:, 4096 * i:4096 * (i + 1)].rearrange("p (s c t) -> p s c t", s=2, c=CHUNKS)
                   for i in range(2)]
        xq_t = [region_w[:, 8192 + 512 * i:8192 + 512 * (i + 1)].rearrange("p (c t) -> p c t", c=CHUNKS)
                for i in range(2)]

        region_t = sb("region_t", [P, 8192], F32R)
        x_t = [region_t[:, 4096 * i:4096 * (i + 1)].rearrange("p (s k t) -> p s k t", s=2, k=CHUNKS)
               for i in range(2)]
        wo = region_t[:, 0:4096].rearrange("p (s k n) -> p s k n", s=2, k=CHUNKS)
        wf = region_t[:, 4096:8192].rearrange("p (s k n) -> p s k n", s=2, k=CHUNKS)

        region_o = sb("region_o", [P, 8192])
        qk_raw = region_o[:, 0:4096].rearrange("p (k n) -> p k n", k=CHUNKS)
        v_raw = region_o[:, 4096:6144].rearrange("p (k n) -> p k n", k=CHUNKS)
        rope = region_o[:, 0:2048].rearrange("p (i t) -> p i t", i=4)
        unit = region_o[:, 2048:6144].rearrange("p (i t) -> p i t", i=8)
        square = region_o[:, 6144:7168].rearrange("p (i t) -> p i t", i=2)
        sqsum = region_o[:, 7168:8192].rearrange("p (i t) -> p i t", i=2)
        o_t = region_o[:, :].rearrange("p (c t) -> p c t", c=CHUNKS)

        v = sb("v", [P, TILES, DIM])
        region_m = sb("region_m", [P, 5120])
        x_in = region_m[:, 0:2048].rearrange("p (i n) -> p i n", i=GT)
        x_hat = region_m[:, 2048:3072].rearrange("p (i n) -> p i n", i=2)
        trig = region_m[:, 3072:5120].rearrange("p (i s t) -> p i s t", i=2, s=2)
        prob = region_m[:, 0:3072].rearrange("p (i e t) -> p i e t", i=NPT, e=2)
        o_stage = region_m[:, 3072:4096].rearrange("p (i t) -> p i t", i=2)
        x3 = region_m[:, 0:2048].rearrange("p (i n) -> p i n", i=4)
        x1 = region_m[:, 2048:4096].rearrange("p (i n) -> p i n", i=4)
        y3 = region_m[:, 4096:5120].rearrange("p (i n) -> p i n", i=2)

        normed = sb("normed", [P, 4, GROUP])
        out_stage = normed
        half_h = sb("half_h", [P, 4, GROUP], F32R)
        last_h = region_t[:, 0:2048].rearrange("p (i t) -> p i t", i=4)
        last_n = region_m[:, 0:2048].rearrange("p (i t) -> p i t", i=4)
        stage_w = sb("stage_w", [P, 2, 1024])
        rec_bc = sb("rec_bc", [P, SEQ])
        diag = sb("diag", [P, 2, GROUP])
        ident = sb("ident", [P, P])
        ident_bf = sb("ident_bf", [P, P], BF16)
        ones = sb("ones", [P, P])
        mask = sb("mask", [P, 2, P])
        qkw = sb("qkw", [P, 8])
        ln_bias = sb("ln_bias", [P, 2])
        stats = sb("stats", [P, GT, 6])
        mean_var = sb("mean_var", [P, GT, 2])
        dev = sb("dev", [P, GT])
        rstd = sb("rstd", [P, GT])
        rms_dev = sb("rms_dev", [P, 2, GT])
        rms_rec = sb("rms_rec", [P, 2, GT])
        neg_max = sb("neg_max", [P, 2, TILES])
        max_split = sb("max_split", [P, 2, 2 * PAIRS], F32R)
        max_rows = sb("max_rows", [2 * PAIRS, 2, P], F32R)
        w_fold = region_m[:, 4096:5120].rearrange("p (i n) -> p i n", i=2)
        sums = sb("sums", [P, 64])
        recs = sb("recs", [P, 64])
        below = stage_w[:, 0, 0:DIM].bitcast(BF16).rearrange("p (i n) -> p i n", i=2)
        xq = stage_w[:, 1, 0:DIM].bitcast(BF16).rearrange("p (i n) -> p i n", i=2)

        psum = ctx.enter_context(nc.psum_tensor("psum", [P, 8, 512], F32))
        BANK_XT, BANK_SUMS, BANK_PAIR, BANK_RMS = 0, 1, 2, 6
        BANK_ST, BANK_O = 4, 6
        BANK_WO, BANK_XQ, BANK_FFN = 0, 2, 4

        zero_set, a_zero = steps("zero_set"), arrivals("a_zero", 3)
        const_set, mask_set, ident_cast = steps("const_set"), steps("mask_set"), steps("ident_cast")
        a_const = arrivals("a_const", 2)
        a_w = [[arrivals(f"a_w{part}{k}") for k in range(CHUNKS)] for part in range(2)]
        wv_high, wv_low = steps("wv_high"), steps("wv_low")
        a_x = arrivals("a_x", GT)
        a_trig = [arrivals(f"a_trig{i}", 2) for i in range(2)]
        a_half = [arrivals(f"a_half{i}", 3) for i in range(4)]
        w_high, w_low = steps("w_high"), steps("w_low")
        bn, aggr, ln_dev, ln_rstd, xhat = (steps(n) for n in ("bn", "aggr", "ln_dev", "ln_rstd", "xhat"))
        xtr, xt_high, xt_low = steps("xtr"), steps("xt_high"), steps("xt_low")
        qk_mm, v_mm, v_out = steps("qk_mm"), steps("v_mm"), steps("v_out")
        roped, squared, rotated, sq_added = steps("roped"), steps("squared"), steps("rotated"), steps("sq_added")
        sq_mm, r_dev, r_rec, diag_s, rms_mm = (steps(n) for n in ("sq_mm", "r_dev", "r_rec", "diag_s", "rms_mm"))
        scaled, q_high, q_low, k_low = steps("scaled"), steps("q_high"), steps("q_low"), steps("k_low")

        a_stack = [[arrivals(f"a_stack{i}{half}", 3) for half in range(2)] for i in range(NSTACK)]
        a_ones = [arrivals(f"a_ones{i}") for i in range(NSTACK)]
        a_rows = [arrivals(f"a_rows{i}") for i in range(2)]
        a_stage = [arrivals(f"a_stage{i}", 3) for i in range(2)]
        a_sums, a_recs, a_bc = arrivals("a_sums"), arrivals("a_recs"), arrivals("a_bc", 4)
        a_wraw = [arrivals(f"a_wraw{i}") for i in range(2)]
        a_wraw2 = [arrivals(f"a_wraw2{i}", 2) for i in range(2)]
        filled, score, merged, maxed = (steps(n) for n in ("filled", "score", "merged", "maxed"))
        m_high, m_low, m_tr, m_row = steps("m_high"), steps("m_low"), steps("m_tr"), steps("m_row")
        st, expd, selected, pv, staged = (steps(n) for n in ("st", "expd", "selected", "pv", "staged"))
        recd, o_done = steps("recd"), steps("o_done")
        wo_high, wo_low = steps("wo_high"), steps("wo_low")
        w_tern, w_tr, wf_high, wf_low = steps("w_tern"), steps("w_tr"), steps("wf_high"), steps("wf_low")

        a_x3 = [arrivals(f"a_x3{i}") for i in range(4)]
        a_out = [arrivals(f"a_out{i}") for i in range(4)]
        o_high, o_low, wo_mm, x1_s = steps("o_high"), steps("o_low"), steps("wo_mm"), steps("x1_s")
        bn3, aggr3, dev3, rstd3, y_s, below_s, xq_s = (
            steps(n) for n in ("bn3", "aggr3", "dev3", "rstd3", "y_s", "below_s", "xq_s"))
        xq_tr, xq_out, ffn_mm, out_s = steps("xq_tr"), steps("xq_out"), steps("ffn_mm"), steps("out_s")

        def f32(ap):
            return ap.bitcast(F32)

        x_tiles = x_d.rearrange("(t p) n -> t p n", p=P)
        out_tiles = out_d.rearrange("(t p) n -> t p n", p=P)

        def pair_free(engine, n):
            if n < 2:
                return
            g, p = divmod(n - 2, 6)
            if p < 4:
                roped.wait(engine, 4 * (4 * g + p) + 3)
                squared.wait(engine, 8 * g + 2 * p + 1)
            else:
                v_out.wait(engine, 4 * g + 2 * (p - 4) + 1)

        def w_halves(k):
            for half in range(2):
                yield (qk_raw[:, k, :].rearrange("c (g h x f) -> c x g h f", g=4, x=2, f=HALF)[:, half],
                       lambda s, half=half: wqk[:, s, k, :].rearrange(
                           "c (g x h f) -> c x g h f", g=4, x=2, f=HALF)[:, half])

        def high_buffer(n):
            return half_h[:, n % 4, :] if n < 8 * GROUPS - 4 else last_h[:, n % 4, :]

        def low_buffer(n):
            return normed[:, n % 4, :].bitcast(F32R) if n < 8 * GROUPS - 4 else last_n[:, n % 4, :].bitcast(F32R)

        def buffer_free(engine, n):
            if n < 8 * GROUPS - 4:
                a_half[n % 4].wait(engine, n // 4 - 1)

        def low_wait(engine, n):
            if n in LOW_DVE:
                k_low.wait(engine, LOW_DVE.index(n))
            else:
                q_low.wait(engine, n - sum(m < n for m in LOW_DVE))

        def head_pair(n):
            return divmod(n, PAIRS)

        LOW_DVE = [8 * GROUPS - 3, 8 * GROUPS - 1]

        M_TR = {4 * c + 5: c for c in range(2 * HEADS)}
        TERN = [30, 38, 46, 54]
        W_TR = {TERN[i // 2] + 2 + 2 * (i % 2): i for i in range(8)}
        STAGED = {4 * c + 4 + PV_LAG: c for c in range(2 * HEADS)}
        RECIP = {32 * c + 32 + 20: c for c in range(CHUNKS)}
        NORM = {32 * c + 32 + 30: c for c in range(CHUNKS)}
        LAST = STEPS + 32
        WO_S = [8, 12, 16, 20]

        block = ctx.enter_context(nc.Block())

        @block.sync
        def _(eng):
            def load_x(g):
                for i in range(GT):
                    a_x.sent(eng.dma_start(x_in[:, i, :], x_tiles[GT * g + i]))

            def load_trig(g):
                cols = slice(GROUP * g, GROUP * (g + 1))
                a_trig[g % 2].sent(eng.dma_start(trig[:, g % 2, 0, :], cos_d[:, cols]))
                a_trig[g % 2].sent(eng.dma_start(trig[:, g % 2, 1, :], sin_d[:, cols]))

            def store_half(g, c):
                n = 8 * g + c
                qk, hg, half = c // 4, (c // 2) % 2, c % 2
                for s in range(3):
                    high = s != (1 if qk else 2)
                    if s == 0:
                        q_high.wait(eng, n)
                        low_wait(eng, n)
                    dst = qk_scr[qk, 8 * hg:8 * hg + 8, s, HALF * half:HALF * (half + 1),
                                 GROUP * g:GROUP * (g + 1)]
                    a_half[n % 4].sent(eng.dma_start(dst, f32(high_buffer(n) if high else low_buffer(n))))

            load_x(0)
            for dst, src in ((ident, ident_d), (qkw, qkw_d)):
                a_const.sent(eng.dma_start(dst[:, :], src))
            for k in range(CHUNKS):
                a_w[0][k].sent(eng.dma_start(qk_raw[:, k, :], wqkv_d[P * k:P * (k + 1), 0:2 * DIM]))
            load_trig(0)
            for k in range(CHUNKS):
                a_w[1][k].sent(eng.dma_start(v_raw[:, k, :], wqkv_d[P * k:P * (k + 1), 2 * DIM:3 * DIM]))
            zero_set.wait(eng, 0)
            rest = P - STACKED
            a_zero.sent(eng.dma_start(zero_scr, rec_bc[0:rest, :]))
            a_zero.sent(eng.dma_start(ones_scr[MAXROWS:rest, :], rec_bc[0:rest - MAXROWS, :]))
            const_set.wait(eng, 3)
            a_zero.sent(eng.dma_start(ones_scr[0:MAXROWS, :].rearrange("r (b t) -> (r b) t", t=P),
                                      ones[0:MAXROWS * SEQ // P, :]))
            xhat.wait(eng, GT - 1)
            load_x(1)
            for g in range(GROUPS):
                if g + 1 < GROUPS:
                    roped.wait(eng, 16 * (g - 1) + 15)
                    load_trig(g + 1)
                if g:
                    for c in range(4, 8):
                        store_half(g - 1, c)
                if g + 2 < GROUPS:
                    xhat.wait(eng, GT * (g + 1) + 3)
                    load_x(g + 2)
                if g + 1 < GROUPS:
                    for c in range(4):
                        store_half(g, c)

            def load_stack(h, half):
                i = h % NSTACK
                cols = slice(1024 * half, 1024 * (half + 1))
                if h >= NSTACK:
                    st.wait(eng, TILES * (h - NSTACK) + TILES // 2 * (half + 1) - 1)
                    rows = STACKED + MAXROWS
                else:
                    rows = P
                    a_zero.wait(eng, 0)
                    if i < 2:
                        qk_mm.wait(eng, 8 * GROUPS - 1)
                    else:
                        v_mm.wait(eng, TILES - 1)
                    if half == 0:
                        a_ones[i].sent(eng.dma_start(f32(k_stack[i][STACKED:P, :]), ones_scr))
                a_stack[i][half].sent(eng.dma_start(f32(q_stack[i][STACKED:rows, cols]),
                                                    zero_scr[0:rows - STACKED, cols]))
                for qk, stack in ((0, q_stack), (1, k_stack)):
                    a_stack[i][half].sent(eng.dma_start(f32(stack[i][0:STACKED, cols]),
                                                        qk_scr[qk, h].rearrange("s d t -> (s d) t")[:, cols]))

            def load_wo(k):
                if k >= 2:
                    wo_low.wait(eng, k - 2)
                a_wraw[k % 2].sent(eng.dma_start(stage_w[:, k % 2, 0:DIM], wo_d[P * k:P * (k + 1), :]))

            for i in range(4):
                a_half[i].wait(eng, 2 * (GROUPS // 2) - 1)
            load_stack(0, 0)
            load_stack(1, 0)
            for c in range(6):
                store_half(GROUPS - 1, c)
            for i in range(2):
                a_half[i].wait(eng, 2 * GROUPS - 1)
            load_stack(0, 1)
            for c in range(6, 8):
                store_half(GROUPS - 1, c)
            load_stack(1, 1)
            for k in range(2):
                load_wo(k)
            for i in range(2, 4):
                a_half[i].wait(eng, 2 * GROUPS - 1)
            for s in range(LAST):
                if s in (3, 8):
                    load_stack(2, (3, 8).index(s))
                if s in M_TR:
                    c = M_TR[s]
                    h, half = divmod(c, 2)
                    m_row.wait(eng, c)
                    dst = q_stack[h % NSTACK][STACKED:STACKED + MAXROWS, 1024 * half:1024 * (half + 1)]
                    a_rows[c % 2].sent(eng.dma_start(f32(dst), f32(max_rows[:, c % 2, :])))
                if s % PAIRS == 6 and NSTACK <= s // PAIRS + 2 < HEADS:
                    load_stack(s // PAIRS + 2, 0)
                if s % PAIRS == 2 and NSTACK <= s // PAIRS + 1 < HEADS:
                    load_stack(s // PAIRS + 1, 1)
                if s in STAGED:
                    c = STAGED[s]
                    h, half = divmod(c, 2)
                    staged.wait(eng, c)
                    tokens = slice(1024 * half, 1024 * (half + 1))
                    rows = HEAD_DIM * (h % 4)
                    for e in range(2):
                        dst = o_t[rows:rows + HEAD_DIM, h // 4, tokens].rearrange("p (j e t) -> p e j t", e=2, t=P)
                        src = o_stage[64 * e:64 * e + HEAD_DIM, c % 2, :].rearrange("p (j t) -> p j t", t=P)
                        a_stage[c % 2].sent(eng.dma_start(dst[:, e], src))
                    dst = sum_scr[h, tokens].rearrange("(j e t) -> e j t", e=2, t=P)
                    src = o_stage[HEAD_DIM:HEAD_DIM + 65:64, c % 2, :].rearrange("p (j t) -> p j t", t=P)
                    a_stage[c % 2].sent(eng.dma_start(dst, src))
                if s + 5 in RECIP:
                    c = RECIP[s + 5]
                    for i in range(2):
                        a_stage[i].wait(eng, 4 * c + 3)
                    a_sums.sent(eng.dma_start(sums[:, :], sum_scr[4 * c:4 * c + 4, :].rearrange(
                        "h (i t) -> (h i) t", t=64)))
                if s - 1 in RECIP:
                    c = RECIP[s - 1]
                    recd.wait(eng, c)
                    a_recs.sent(eng.dma_start(rec_scr[4 * c:4 * c + 4, :].rearrange("h (i t) -> (h i) t", t=64),
                                              recs[:, :]))
                if s - 4 in RECIP:
                    c = RECIP[s - 4]
                    a_recs.wait(eng, c)
                    if c:
                        o_done.wait(eng, c - 1)
                    for h in range(4):
                        a_bc.sent(eng.dma_start(rec_bc[HEAD_DIM * h:HEAD_DIM * (h + 1), :],
                                                rec_scr[4 * c + h:4 * c + h + 1, :].to_broadcast([HEAD_DIM, SEQ])))
                if s + 6 in WO_S[2:]:
                    load_wo(WO_S.index(s + 6))
                if s + 8 in TERN:
                    k = TERN.index(s + 8)
                    if k == 0:
                        wo_low.wait(eng, 3)
                    if k >= 2:
                        w_tern.wait(eng, 4 * (k - 2) + 3)
                    a_wraw2[k % 2].sent(eng.dma_start(stage_w[:, k % 2, 0:DIM], wf_d[P * k:P * (k + 1), :]))
                    a_wraw2[k % 2].sent(eng.dma_start(stage_w[:, k % 2, DIM:2 * DIM], rram_d[P * k:P * (k + 1), :]))

            expd.wait(eng, 2 * STEPS - 1)
            selected.wait(eng, 2 * STEPS - HEADS - 1)
            pv.wait(eng, STEPS - 1)
            def load_x3(t):
                if t >= 4:
                    x1_s.wait(eng, t - 4)
                a_x3[t % 4].sent(eng.dma_start(x3[:, t % 4, :], x_tiles[t]))
            for t in range(4):
                load_x3(t)
            for t in range(TILES):
                if t + 4 < TILES:
                    load_x3(t + 4)
                if t >= 3:
                    out_s.wait(eng, t - 3)
                    a_out[(t - 3) % 4].sent(eng.dma_start(out_tiles[t - 3], out_stage[:, (t - 3) % 4, :]))
            for t in range(TILES - 3, TILES):
                out_s.wait(eng, t)
                a_out[t % 4].sent(eng.dma_start(out_tiles[t], out_stage[:, t % 4, :]))
            for i in range(4):
                a_out[i].wait(eng, TILES // 4 - 1)

        @block.tensor
        def _(eng):
            SPLIT = ((0, 0), (0, 1), (1, 0))

            def transpose_x(t):
                xhat.wait(eng, t)
                xt_high.wait(eng, t - 1)
                xt_low.wait(eng, t - 1)
                for k in range(CHUNKS):
                    last = nc.tensor.transpose(psum[:, BANK_XT, P * k:P * (k + 1)],
                                               x_hat[:, t % 2, P * k:P * (k + 1)], ident[:, :])
                xtr.done(last)

            def project_qk(g, p):
                n = 6 * g + p
                pair_free(eng, n)
                order = [(half, k) for half in range(2) for k in range(CHUNKS)]
                if n == 0:
                    order = [(half, k) for k in range(CHUNKS) for half in range(2)]
                for half, k in order:
                    if n == 0 and half == 0:
                        w_high.wait(eng, 2 * k + 1)
                        w_low.wait(eng, 2 * k + 1)
                    for a, b in SPLIT:
                        w = wqk[:, a, k, 256 * p + P * half:256 * p + P * (half + 1)]
                        last = nc.tensor.matmul(psum[:, BANK_PAIR + 2 * (n % 2) + half, :], w,
                                                x_t[g % 2][:, b, k, :], start=(k == 0 and a + b == 0),
                                                stop=(k == CHUNKS - 1 and a == 1))
                    if k == CHUNKS - 1:
                        qk_mm.done(last)

            def project_v(g, p):
                n = 6 * g + 4 + p
                pair_free(eng, n)
                if g == 0:
                    wv_high.wait(eng, CHUNKS - 1)
                    wv_low.wait(eng, CHUNKS - 1)
                for e in range(2):
                    i = 2 * p + e
                    out = psum[:, BANK_PAIR + 2 * (n % 2) + e, :]
                    j = 0
                    for k in range(CHUNKS):
                        for a, b in SPLIT:
                            last = nc.tensor.matmul(out, x_t[g % 2][:, b, k, P * i:P * (i + 1)],
                                                    wv[:, a, k, :], start=(j == 0), stop=(j == 11))
                            j += 1
                    v_mm.done(last)

            def sum_squares(g, s):
                sq_added.wait(eng, 6 * g + 3 * s + 2)
                r_dev.wait(eng, 2 * g + s - 1)
                for i in range(GT):
                    last = nc.tensor.matmul(psum[:, BANK_SUMS, i:i + 1], sqsum[:, s, P * i:P * (i + 1)],
                                            ones[:, 0:1], start=True, stop=True)
                sq_mm.done(last)

            def spread_rms(g, s):
                diag_s.wait(eng, GT * (2 * g + s) + GT - 1)
                if g:
                    scaled.wait(eng, 8 * (g - 1) + 4 * s + 3)
                rms_mm.done(nc.tensor.matmul(psum[:, BANK_RMS + s, :], ones[:, :], diag[:, s, :],
                                             start=True, stop=True))

            a_const.wait(eng, 0)
            const_set.wait(eng, 3)
            for t in range(GT):
                transpose_x(t)
            for g in range(GROUPS):
                xt_high.wait(eng, GT * g + 3)
                xt_low.wait(eng, GT * g + 3)
                for p in range(4):
                    project_qk(g, p)
                    if p == 2:
                        sum_squares(g, 0)
                    if g + 1 < GROUPS:
                        transpose_x(GT * (g + 1) + p)
                spread_rms(g, 0)
                project_v(g, 0)
                sum_squares(g, 1)
                project_v(g, 1)
                spread_rms(g, 1)

            def scores(n):
                h, j = head_pair(n)
                if j == 0:
                    filled.wait(eng, h)
                    a_ones[h % NSTACK].wait(eng, 0)
                if j % 4 == 0:
                    a_stack[h % NSTACK][j // 4].wait(eng, h // NSTACK)
                if n >= 2:
                    maxed.wait(eng, n - 2)
                elif n == 0:
                    r_dev.wait(eng, 2 * GROUPS - 1)
                    xt_low.wait(eng, TILES - 1)
                else:
                    v_out.wait(eng, TILES - 3)
                qs, ks = q_stack[h % NSTACK], k_stack[h % NSTACK]
                for e in range(2):
                    qt = 2 * j + e
                    k0 = max(0, qt - 2)
                    last = nc.tensor.matmul(psum[:, 2 * (n % 2) + e, P * (k0 - qt + 2):3 * P],
                                            qs[:, P * qt:P * (qt + 1)],
                                            ks[:, P * k0:P * (qt + 1)], start=True, stop=True)
                score.done(last)

            def maxima_to_rows(c, s):
                m_low.wait(eng, c)
                m_tr.done(nc.tensor.transpose(psum[0:2 * PAIRS, 2 * (s % 2), 3 * P:4 * P],
                                              f32(max_split[:, c % 2, :]), ident[:, :]))

            def transpose_w(i):
                k, d0 = divmod(i, 2)
                w_tern.wait(eng, 4 * k + 3)
                return k, 2 * d0

            def scores_t(n):
                h, j = head_pair(n)
                c = 2 * h + min(2 * j + 3, TILES - 1) // PAIRS
                a_rows[c % 2].wait(eng, c // 2)
                if n == 0:
                    v_out.wait(eng, TILES - 1)
                qs, ks = q_stack[h % NSTACK], k_stack[h % NSTACK]
                for e in range(2):
                    kt = 2 * j + e
                    expd.wait(eng, 2 * (n - 1) + e)
                    q1 = min(TILES, kt + 3)
                    last = nc.tensor.matmul(psum[:, BANK_ST + e, 0:P * (q1 - kt)],
                                            ks[:, P * kt:P * (kt + 1)],
                                            qs[:, P * kt:P * q1], start=True, stop=True)
                    st.done(last)

            def times_v(n):
                h, j = head_pair(n)
                c = n // 4
                selected.wait(eng, (2 * PAIRS - 1) * h + min(2 * j + 1, 2 * PAIRS - 2))
                if n % 4 == 0:
                    staged.wait(eng, c - 2)
                    if n == 0:
                        scaled.wait(eng, 8 * GROUPS - 1)
                cols = slice(P * (n % 4), P * (n % 4 + 1))
                for b in range(3):
                    for e in range(2):
                        qt = 2 * j + e
                        kt = qt - 2 + b
                        if kt < 0:
                            continue
                        probs = prob[:, (n - j + kt // 2) % NPT, kt % 2, P * (qt - kt):P * (qt - kt + 1)]
                        for r, w in ((2 * e, v[:, kt, HEAD_DIM * h:HEAD_DIM * (h + 1)]),
                                     (2 * e + 1, ones[:, 0:HEAD_DIM])):
                            last = nc.tensor.matmul(psum[32 * r:32 * r + 32, BANK_O + c % 2, cols], w, probs,
                                                    start=(kt == max(0, qt - 2)), stop=(kt == qt),
                                                    tile_position=(0, 32 * r))
                pv.done(last)

            for s in range(STEPS + PV_LAG):
                if 0 <= s - ST_LAG < STEPS:
                    scores_t(s - ST_LAG)
                if s < STEPS:
                    scores(s)
                else:
                    if s - 2 < STEPS:
                        maxed.wait(eng, s - 2)
                if s in M_TR:
                    maxima_to_rows(M_TR[s], s)
                if s in W_TR:
                    k, d0 = transpose_w(W_TR[s])
                    for e in range(2):
                        last = nc.tensor.transpose(psum[:, 2 * (s % 2) + e, 3 * P:4 * P],
                                                   w_fold[:, k % 2, P * (d0 + e):P * (d0 + e + 1)], ident[:, :])
                    w_tr.done(last)
                if 0 <= s - PV_LAG < STEPS:
                    times_v(s - PV_LAG)

            def project_o(t):
                g, i = divmod(t, GT)
                o_high.wait(eng, CHUNKS * g + CHUNKS - 1)
                o_low.wait(eng, CHUNKS * g + CHUNKS - 1)
                if t == 0:
                    wo_high.wait(eng, CHUNKS - 1)
                    wo_low.wait(eng, CHUNKS - 1)
                    m_row.wait(eng, 2 * HEADS - 1)
                if t >= 2:
                    x1_s.wait(eng, t - 2)
                else:
                    maxed.wait(eng, STEPS - 2 + t)
                j = 0
                for c in range(CHUNKS):
                    for a, b in SPLIT:
                        last = nc.tensor.matmul(psum[:, BANK_WO + t % 2, :],
                                                o_split[g % 2][:, a, c, P * i:P * (i + 1)], wo[:, b, c, :],
                                                start=(j == 0), stop=(j == 11))
                        j += 1
                wo_mm.done(last)

            def transpose_xq(t):
                xq_s.wait(eng, t)
                xq_out.wait(eng, t - 2)
                for c in range(CHUNKS):
                    last = nc.tensor.transpose(psum[:, BANK_XQ + t % 2, 0:DIM // 2].bitcast(BF16)[:, P * c:P * (c + 1)],
                                               xq[:, t % 2, P * c:P * (c + 1)], ident_bf[:, :])
                xq_tr.done(last)

            def ffn(t):
                xq_out.wait(eng, t)
                if t == 0:
                    wf_low.wait(eng, 15)
                if t >= 2:
                    out_s.wait(eng, t - 2)
                else:
                    expd.wait(eng, 2 * STEPS - 1)
                j = 0
                for c in range(CHUNKS):
                    for a in range(2):
                        last = nc.tensor.matmul(psum[:, BANK_FFN + t % 2, :], xq_t[t % 2][:, c, :], wf[:, a, c, :],
                                                start=(j == 0), stop=(j == 7))
                        j += 1
                ffn_mm.done(last)

            for t in range(TILES + 3):
                if t < TILES:
                    project_o(t)
                if 0 <= t - 2 < TILES:
                    transpose_xq(t - 2)
                if 0 <= t - 3 < TILES:
                    ffn(t - 3)

        @block.scalar
        def _(eng):
            const_set.wait(eng, 3)

            def ln_sqrt(g):
                aggr.wait(eng, GT * g + 3)
                ln_rstd.wait(eng, g - 1)
                ln_dev.done(nc.scalar.activation(dev[:, :], mean_var[:, :, 1], ACT.Sqrt, bias=ln_bias[:, 0:1]))

            def high_x(t):
                xtr.wait(eng, t)
                g, i = divmod(t, GT)
                if g >= 2:
                    v_mm.wait(eng, GT * (g - 2) + 3)
                xt_high.done(nc.scalar.copy(x_t[g % 2][:, 0, :, P * i:P * (i + 1)],
                                            psum[:, BANK_XT, :].rearrange("p (k t) -> p k t", k=CHUNKS)))

            def squares(g, p):
                for half in range(2):
                    c = 2 * p + half
                    qk_mm.wait(eng, 8 * g + c)
                    m = 4 * g + p - 1
                    if m >= 0:
                        sq_added.wait(eng, 3 * (m // 2) + (0 if m % 2 == 0 else 2))
                    squared.done(nc.scalar.activation(square[:, half, :],
                                                      psum[:, BANK_PAIR + 2 * ((6 * g + p) % 2) + half, :],
                                                      ACT.Square))

            def rms_sqrt(g, s):
                m = 2 * g + s
                sq_mm.wait(eng, m)
                if g:
                    r_rec.wait(eng, m - 2)
                r_dev.done(nc.scalar.activation(rms_dev[:, s, :], psum[:, BANK_SUMS, 0:GT], ACT.Sqrt,
                                                bias=ln_bias[:, 1:2], scale=1.0 / DIM))

            def evacuate_v(g, p, e):
                t = GT * g + 2 * p + e
                v_mm.wait(eng, t)
                v_out.done(nc.scalar.copy(v[:, t, :], psum[:, BANK_PAIR + 2 * ((6 * g + 4 + p) % 2) + e, :]))

            def high_qk(g, c):
                n = 8 * g + c
                scaled.wait(eng, n)
                buffer_free(eng, n)
                q_high.done(nc.scalar.copy(high_buffer(n), f32(low_buffer(n))))

            ln_sqrt(0)
            for k in range(CHUNKS):
                high_x(k)
                a_w[0][k].wait(eng, 0)
                for raw, kept in w_halves(k):
                    w_high.done(nc.scalar.copy(kept(0), raw))
            for g in range(GROUPS):
                if g + 1 < GROUPS:
                    ln_sqrt(g + 1)
                for p in range(4):
                    squares(g, p)
                    if p == 2:
                        rms_sqrt(g, 0)
                    if g + 1 < GROUPS:
                        high_x(GT * (g + 1) + p)
                    if p < 2 and g:
                        high_qk(g - 1, 4 + 2 * p)
                        high_qk(g - 1, 5 + 2 * p)
                    if p == 1 and g == 0:
                        for k in range(CHUNKS):
                            a_w[1][k].wait(eng, 0)
                            wv_high.done(nc.scalar.copy(wv[:, 0, k, :], v_raw[:, k, :]))
                for e in range(2):
                    evacuate_v(g, 0, e)
                    high_qk(g, 2 * e)
                    high_qk(g, 2 * e + 1)
                rms_sqrt(g, 1)
                for e in range(2):
                    evacuate_v(g, 1, e)
            for c in range(4, 8):
                high_qk(GROUPS - 1, c)

            def exponentials(n):
                h, j = head_pair(n)
                pv.wait(eng, n - 3)
                if n == 0:
                    xtr.wait(eng, TILES - 1)
                    roped.wait(eng, 16 * GROUPS - 1)
                for e in range(2):
                    st.wait(eng, 2 * n + e)
                    cols = P * min(3, TILES - 2 * j - e)
                    expd.done(nc.scalar.activation(prob[:, n % NPT, e, 0:cols], psum[:, BANK_ST + e, 0:cols],
                                                   ACT.Exp, scale=SCALE))

            def stage(c):
                pv.wait(eng, 4 * c + 3)
                if c >= 2:
                    a_stage[c % 2].wait(eng, c // 2 - 1)
                staged.done(nc.scalar.copy(o_stage[:, c % 2, :], psum[:, BANK_O + c % 2, :]))

            for s in range(STEPS + PV_LAG + 2):
                if 0 <= s - ST_LAG < STEPS:
                    exponentials(s - ST_LAG)
                if s in STAGED:
                    stage(STAGED[s])
                if s in WO_S:
                    k = WO_S.index(s)
                    if k == 0:
                        for i in range(4):
                            a_half[i].wait(eng, 2 * GROUPS - 1)
                    a_wraw[k % 2].wait(eng, k // 2)
                    wo_high.done(nc.scalar.copy(wo[:, 0, k, :], stage_w[:, k % 2, 0:DIM]))

            def high_o(g):
                for c in range(CHUNKS):
                    o_done.wait(eng, c)
                    if g == 0 and c == 0:
                        st.wait(eng, 2 * STEPS - 1)
                    if g >= 2:
                        wo_mm.wait(eng, GT * (g - 2) + 3)
                    o_high.done(nc.scalar.copy(o_split[g % 2][:, 0, c, :], o_t[:, c, GROUP * g:GROUP * (g + 1)]))

            high_o(0)
            for t in range(TILES + 2):
                if t < TILES:
                    if t % GT == 1 and t // GT + 1 < GROUPS:
                        high_o(t // GT + 1)
                    aggr3.wait(eng, t)
                    rstd3.wait(eng, t - 4)
                    dev3.done(nc.scalar.activation(dev[:, t % 4:t % 4 + 1], mean_var[:, t % 4, 1:2], ACT.Sqrt,
                                                   bias=ln_bias[:, 0:1]))
                if 0 <= t - 2 < TILES:
                    u = t - 2
                    xq_tr.wait(eng, u)
                    ffn_mm.wait(eng, u - 2)
                    xq_out.done(nc.scalar.copy(
                        xq_t[u % 2][:, :, :],
                        psum[:, BANK_XQ + u % 2, 0:DIM // 2].bitcast(BF16).rearrange("p (c t) -> p c t", c=CHUNKS)))

        @block.gpsimd
        def _(eng):
            const_set.done(nc.gpsimd.memset(ones[:, :], 1.0))
            const_set.done(nc.gpsimd.memset(ln_bias[:, 0:1], LN_EPS))
            const_set.done(nc.gpsimd.memset(ln_bias[:, 1:2], RMS_EPS))
            const_set.done(nc.gpsimd.memset(mask[:, :, :], 1.0))
            zero_set.done(nc.gpsimd.memset(rec_bc[:, :], 0.0))
            const_set.wait(eng, 3)
            mask_set.done(nc.gpsimd.affine_select(out=mask[:, :, :], in_=mask[:, :, :], compare_op=ALU.is_ge,
                                                  fill=0.0, base=0, pattern=[[0, 2], [-1, P]],
                                                  channel_multiplier=1))

            def rotate(g, p):
                m = 4 * g + p
                u = 4 * (p // 2) + 2 * (p % 2)
                if g:
                    scaled.wait(eng, 8 * (g - 1) + 2 * p + 1)
                roped.wait(eng, 4 * m + 1)
                rotated.done(nc.gpsimd.tensor_tensor(unit[:, u, :], rope[:, 0, :], rope[:, 1, :], ALU.subtract))
                roped.wait(eng, 4 * m + 3)
                rotated.done(nc.gpsimd.tensor_tensor(unit[:, u + 1, :], rope[:, 2, :], rope[:, 3, :], ALU.add))

            def add_squares(g, p):
                s = p // 2
                squared.wait(eng, 8 * g + 2 * p + 1)
                if p % 2 == 0:
                    if g:
                        sq_mm.wait(eng, 2 * (g - 1) + s)
                    sq_added.done(nc.gpsimd.tensor_tensor(sqsum[:, s, :], square[:, 0, :], square[:, 1, :], ALU.add))
                else:
                    for half in range(2):
                        n = 6 * g + 3 * s + 1 + half
                        sq_added.wait(eng, n - 1)
                        sq_added.done(nc.gpsimd.tensor_tensor(sqsum[:, s, :], sqsum[:, s, :], square[:, half, :],
                                                              ALU.add))

            def low_qk(g, c):
                n = 8 * g + c
                if n not in LOW_DVE:
                    q_high.wait(eng, n)
                    q_low.done(nc.gpsimd.tensor_tensor(low_buffer(n), f32(low_buffer(n)), f32(high_buffer(n)),
                                                       ALU.subtract))

            for g in range(GROUPS):
                for p in range(4):
                    add_squares(g, p)
                    rotate(g, p)
                    if p < 2 and g:
                        low_qk(g - 1, 4 + 2 * p)
                        low_qk(g - 1, 5 + 2 * p)
                for c in range(4):
                    low_qk(g, c)
            for c in range(4, 8):
                low_qk(GROUPS - 1, c)

            for n in range(STEPS):
                h, j = head_pair(n)
                expd.wait(eng, 2 * n + 1)
                near = prob[:, n % NPT, :, 0:P]
                selected.done(nc.gpsimd.affine_select(out=near, in_=near, compare_op=ALU.is_ge, fill=0.0, base=0,
                                                      pattern=[[0, 2], [1, P]], channel_multiplier=-1))
                if j < PAIRS - 1:
                    far = prob[:, n % NPT, :, 2 * P:3 * P]
                    selected.done(nc.gpsimd.affine_select(out=far, in_=far, compare_op=ALU.is_ge, fill=0.0,
                                                          base=WINDOW - 1 - 2 * P, pattern=[[0, 2], [-1, P]],
                                                          channel_multiplier=1))

            for g in range(GROUPS):
                for c in range(CHUNKS):
                    o_high.wait(eng, CHUNKS * g + c)
                    o_low.done(nc.gpsimd.tensor_tensor(o_split[g % 2][:, 1, c, :], o_t[:, c, GROUP * g:GROUP * (g + 1)],
                                                       f32(o_split[g % 2][:, 0, c, :]), ALU.subtract))

        @block.vector
        def _(eng):
            vec = nc.vector

            def ln_stats(g):
                for i in range(GT):
                    a_x.wait(eng, g)
                    xhat.wait(eng, GT * (g - 1) + i)
                    bn.done(vec.bn_stats(stats[:, i, :], x_in[:, i, :]))
                for i in range(GT):
                    bn.wait(eng, GT * g + i)
                    aggr.done(vec.bn_aggr(mean_var[:, i, :], stats[:, i, :]))

            def ln_recip(g):
                ln_dev.wait(eng, g)
                ln_rstd.done(vec.reciprocal(rstd[:, :], dev[:, :]))

            def normalise(t):
                g, i = divmod(t, GT)
                ln_rstd.wait(eng, g)
                xtr.wait(eng, t - 2)
                xhat.done(vec.tensor_scalar(x_hat[:, t % 2, :], x_in[:, i, :], mean_var[:, i, 0:1],
                                            rstd[:, i:i + 1], ALU.subtract, ALU.mult))

            def low_x(t):
                g, i = divmod(t, GT)
                xt_high.wait(eng, t)
                xt_low.done(vec.tensor_tensor(x_t[g % 2][:, 1, :, P * i:P * (i + 1)],
                                              psum[:, BANK_XT, :].rearrange("p (k t) -> p k t", k=CHUNKS),
                                              f32(x_t[g % 2][:, 0, :, P * i:P * (i + 1)]), ALU.subtract))

            def rope_products(g, p):
                m = 4 * g + p
                banks = BANK_PAIR + 2 * ((6 * g + p) % 2)
                squared.wait(eng, 8 * g + 2 * p + 1)
                a_trig[g % 2].wait(eng, g // 2)
                for i, (half, s) in enumerate(((0, 0), (1, 1), (1, 0), (0, 1))):
                    if m:
                        rotated.wait(eng, 2 * (m - 1) + i // 2)
                    roped.done(vec.scalar_tensor_tensor(rope[:, i, :], psum[:, banks + half, :],
                                                        qkw[:, 2 * p + half:2 * p + half + 1],
                                                        trig[:, g % 2, s, :], ALU.mult, ALU.mult))

            def rms_recip(g, s):
                m = 2 * g + s
                r_dev.wait(eng, m)
                r_rec.done(vec.reciprocal(rms_rec[:, s, :], rms_dev[:, s, :]))
                r_rec.wait(eng, m)
                if g:
                    rms_mm.wait(eng, m - 2)
                for i in range(GT):
                    diag_s.done(vec.tensor_scalar(diag[:, s, P * i:P * (i + 1)], ident[:, :],
                                                  rms_rec[:, s, i:i + 1], None, ALU.mult))

            def scale_qk(g, c):
                n, s = 8 * g + c, c // 4
                rms_mm.wait(eng, 2 * g + s)
                rotated.wait(eng, n)
                buffer_free(eng, n)
                scaled.done(vec.tensor_tensor(f32(low_buffer(n)), unit[:, c, :], psum[:, BANK_RMS + s, :],
                                              ALU.mult))

            def low_w(k):
                for i, (raw, kept) in enumerate(w_halves(k)):
                    w_high.wait(eng, 2 * k + i)
                    w_low.done(vec.tensor_tensor(kept(1), raw, f32(kept(0)), ALU.subtract))

            a_const.wait(eng, 0)
            ident_cast.done(vec.tensor_copy(ident_bf[:, :], ident[:, :]))
            ln_stats(0)
            ln_recip(0)
            normalise(0)
            normalise(1)
            for k in range(CHUNKS):
                low_x(k)
                if k < 2:
                    normalise(2 + k)
                low_w(k)
            for g in range(GROUPS):
                more = g + 1 < GROUPS
                t = GT * (g + 1)
                if more:
                    ln_stats(g + 1)
                    ln_recip(g + 1)
                    normalise(t)
                    normalise(t + 1)
                for p in range(4):
                    rope_products(g, p)
                    if more:
                        low_x(t + p)
                        if p < 2:
                            normalise(t + 2 + p)
                    if p < 2 and g:
                        scale_qk(g - 1, 4 + 2 * p)
                        scale_qk(g - 1, 5 + 2 * p)
                    if p == 1 and g == 0:
                        for k in range(CHUNKS):
                            wv_high.wait(eng, k)
                            wv_low.done(vec.tensor_tensor(wv[:, 1, k, :], v_raw[:, k, :], f32(wv[:, 0, k, :]),
                                                          ALU.subtract))
                    if p == 2:
                        rms_recip(g, 0)
                for c in range(4):
                    scale_qk(g, c)
                rms_recip(g, 1)
            for c in range(4, 8):
                scale_qk(GROUPS - 1, c)
                n = 8 * (GROUPS - 1) + c
                if n in LOW_DVE:
                    q_high.wait(eng, n)
                    k_low.done(vec.tensor_tensor(low_buffer(n), f32(low_buffer(n)), f32(high_buffer(n)),
                                                 ALU.subtract))

            def fill(h):
                if h == 0:
                    r_dev.wait(eng, 2 * GROUPS - 1)
                else:
                    maxed.wait(eng, PAIRS * h - 2)
                filled.done(vec.memset(psum[:, 0:2, 0:P], LOWEST))

            def merge(n):
                score.wait(eng, n)
                if n in M_TR:
                    m_tr.wait(eng, M_TR[n])
                if n in W_TR:
                    w_tr.wait(eng, W_TR[n])
                merged.done(vec.copy_predicated(psum[:, 2 * (n % 2):2 * (n % 2) + 2, 0:P], mask[:, :, :].bitcast(U32),
                                                psum[:, 2 * (n % 2):2 * (n % 2) + 2, 2 * P:3 * P]))

            def maximum(n):
                h, j = head_pair(n)
                slot = 2 * (n % 2)
                merged.wait(eng, n)
                if h >= 2:
                    m_low.wait(eng, 2 * (h - 2) + j // 4)
                if j == 0:
                    vec.tensor_reduce(neg_max[:, h % 2, 0:1], psum[:, slot, 0:P], axis=AX_X, op=ALU.max, negate=True)
                    maxed.done(vec.tensor_reduce(neg_max[:, h % 2, 1:2], psum[:, slot + 1, 0:2 * P], axis=AX_X,
                                                 op=ALU.max, negate=True))
                else:
                    maxed.done(vec.tensor_reduce(neg_max[:, h % 2, 2 * j:2 * j + 2], psum[:, slot:slot + 2, 0:2 * P],
                                                 axis=AX_X, op=ALU.max, negate=True))

            def split_maxima(c):
                h, half = divmod(c, 2)
                maxed.wait(eng, 4 * c + 3)
                if c >= 2:
                    m_tr.wait(eng, c - 2)
                cols = neg_max[:, h % 2, PAIRS * half:PAIRS * (half + 1)]
                m_high.done(vec.tensor_copy(max_split[:, c % 2, 0:PAIRS], cols))
                m_high.wait(eng, c)
                m_low.done(vec.tensor_tensor(max_split[:, c % 2, PAIRS:2 * PAIRS], cols,
                                             f32(max_split[:, c % 2, 0:PAIRS]), ALU.subtract))

            def evacuate_rows(c, s):
                m_tr.wait(eng, c)
                if c >= 2:
                    a_rows[c % 2].wait(eng, c // 2 - 1)
                m_row.done(vec.tensor_copy(max_rows[:, c % 2, :], psum[0:2 * PAIRS, 2 * (s % 2), 3 * P:4 * P]))

            def ternary_w(k):
                a_wraw2[k % 2].wait(eng, k // 2)
                if k >= 2:
                    w_tr.wait(eng, 2 * (k - 2) + 1)
                w, var, fold = stage_w[:, k % 2, 0:DIM], stage_w[:, k % 2, DIM:2 * DIM], w_fold[:, k % 2, :]
                w_tern.done(vec.tensor_scalar(fold, w, TH_W, SC_W, ALU.is_gt, ALU.mult))
                w_tern.wait(eng, 4 * k)
                w_tern.done(vec.tensor_scalar(w, w, -TH_W, SC_W, ALU.is_lt, ALU.mult))
                w_tern.wait(eng, 4 * k + 1)
                w_tern.done(vec.tensor_tensor(fold, fold, w, ALU.subtract))
                w_tern.wait(eng, 4 * k + 2)
                w_tern.done(vec.tensor_tensor(fold, fold, var, ALU.add))

            def split_wf(i, s):
                k, d0 = i // 2, 2 * (i % 2)
                w_tr.wait(eng, i)
                for e in range(2):
                    src = psum[:, 2 * (s % 2) + e, 3 * P:4 * P]
                    high = wf[:, 0, d0 + e, P * k:P * (k + 1)]
                    wf_high.done(vec.tensor_scalar(high, src, SC_X, None, ALU.mult))
                    wf_high.wait(eng, 2 * i + e)
                    wf_low.done(vec.scalar_tensor_tensor(wf[:, 1, d0 + e, P * k:P * (k + 1)], src, SC_X, f32(high),
                                                         ALU.mult, ALU.subtract))

            def recip_sums(c):
                a_sums.wait(eng, c)
                if c:
                    a_recs.wait(eng, c - 1)
                recd.done(vec.reciprocal(recs[:, :], sums[:, :]))

            def divide(c):
                a_bc.wait(eng, c)
                o_done.done(vec.tensor_tensor(o_t[:, c, :], o_t[:, c, :], rec_bc[:, :], ALU.mult))

            mask_set.wait(eng, 0)
            fill(0)
            for s in range(LAST):
                if s < STEPS:
                    merge(s)
                if s in M_TR:
                    evacuate_rows(M_TR[s], s)
                if s in W_TR:
                    split_wf(W_TR[s], s)
                if s < STEPS:
                    maximum(s)
                    if s % PAIRS == PAIRS - 2 and s // PAIRS + 1 < HEADS:
                        fill(s // PAIRS + 1)
                    if s % 4 == 3:
                        split_maxima(s // 4)
                if s in WO_S:
                    k = WO_S.index(s)
                    wo_high.wait(eng, k)
                    wo_low.done(vec.tensor_tensor(wo[:, 1, k, :], stage_w[:, k % 2, 0:DIM], f32(wo[:, 0, k, :]),
                                                  ALU.subtract))
                if s in TERN:
                    ternary_w(TERN.index(s))
                if s in RECIP:
                    recip_sums(RECIP[s])
                if s in NORM:
                    divide(NORM[s])

            def residual(t):
                wo_mm.wait(eng, t)
                a_x3[t % 4].wait(eng, t // 4)
                if t >= 4:
                    out_s.wait(eng, t - 4)
                x1_s.done(vec.tensor_tensor(x1[:, t % 4, :], psum[:, BANK_WO + t % 2, :], x3[:, t % 4, :], ALU.add))
                x1_s.wait(eng, t)
                bn3.done(vec.bn_stats(stats[:, t % 4, :], x1[:, t % 4, :]))
                bn3.wait(eng, t)
                y_s.wait(eng, t - 4)
                aggr3.done(vec.bn_aggr(mean_var[:, t % 4, :], stats[:, t % 4, :]))

            def quantise(t):
                dev3.wait(eng, t)
                y_s.wait(eng, t - 4)
                rstd3.done(vec.reciprocal(rstd[:, t % 4:t % 4 + 1], dev[:, t % 4:t % 4 + 1]))
                rstd3.wait(eng, t)
                y = y3[:, t % 2, :]
                y_s.done(vec.tensor_scalar(y, x1[:, t % 4, :], mean_var[:, t % 4, 0:1], rstd[:, t % 4:t % 4 + 1],
                                           ALU.subtract, ALU.mult))
                y_s.wait(eng, t)
                below_s.done(vec.tensor_scalar(below[:, t % 2, :], y, -TH_X, None, ALU.is_lt))
                below_s.wait(eng, t)
                xq_tr.wait(eng, t - 2)
                xq_s.done(vec.scalar_tensor_tensor(xq[:, t % 2, :], y, TH_X, below[:, t % 2, :], ALU.is_gt,
                                                   ALU.subtract))

            def result(t):
                ffn_mm.wait(eng, t)
                if t >= 4:
                    a_out[t % 4].wait(eng, t // 4 - 1)
                out_s.done(vec.tensor_tensor(out_stage[:, t % 4, :], psum[:, BANK_FFN + t % 2, :], x1[:, t % 4, :],
                                             ALU.add))

            for t in range(TILES + 3):
                if t < TILES:
                    residual(t)
                if 0 <= t - 1 < TILES:
                    quantise(t - 1)
                if 0 <= t - 3 < TILES:
                    result(t - 3)


def kernel(L0_attn_hidden_states, L0_attn_Wqkv, L0_attn_q_norm_w, L0_attn_k_norm_w, L0_attn_Wo, L0_ffn_weight,
           L0_ffn_rram_variation):
    import concourse.bacc as bacc
    from concourse.bass_utils import run_bass_kernel_spmd

    f4 = np.float32
    inv_freq = (f4(1.0) / np.power(f4(THETA), np.arange(0, HEAD_DIM, 2, dtype=f4) / f4(HEAD_DIM))).astype(f4)
    angle = (np.arange(SEQ, dtype=f4)[None, :] * inv_freq[:, None]).astype(f4).astype(np.float64)
    cos = np.tile(np.cos(angle).astype(f4), (P // HALF, 1))
    sin = np.tile(np.sin(angle).astype(f4), (P // HALF, 1))

    def by_chunk(w):
        return np.asarray(w).reshape(2, 8, 2, HALF).transpose(1, 3, 0, 2).reshape(P, CHUNKS)

    arrays = {
        "x": np.ascontiguousarray(np.asarray(L0_attn_hidden_states).reshape(SEQ, DIM)),
        "wqkv": np.ascontiguousarray(L0_attn_Wqkv),
        "qkw": np.ascontiguousarray(np.concatenate([by_chunk(L0_attn_q_norm_w), by_chunk(L0_attn_k_norm_w)], 1)),
        "wo": np.ascontiguousarray(L0_attn_Wo),
        "wf": np.ascontiguousarray(L0_ffn_weight),
        "rram": np.ascontiguousarray(L0_ffn_rram_variation),
        "cos": cos, "sin": sin, "ident": np.eye(P, dtype=f4),
    }
    nc = bacc.Bacc("TRN2", target_bir_lowering=False, num_devices=1)
    args = [nc.dram_tensor(f"in_{n}", a.shape, mybir.dt.from_np(a.dtype), kind="ExternalInput").ap()
            for n, a in arrays.items()]
    out = nc.dram_tensor("out", (SEQ, DIM), F32, kind="ExternalOutput").ap()
    build(nc, *args, out)
    result = run_bass_kernel_spmd(nc, [{f"in_{n}": a for n, a in arrays.items()}], core_ids=[0])
    return result.results[0]["out"].reshape(1, SEQ, DIM)
```

```python
from contextlib import ExitStack

import numpy as np

import concourse.bass as bass
from concourse import mybir

F32 = mybir.dt.float32
F32R = mybir.dt.float32r
BF16 = mybir.dt.bfloat16
U32 = mybir.dt.uint32
ALU = mybir.AluOpType
ACT = mybir.ActivationFunctionType
AX_X = mybir.AxisListType.X

P = 128
SEQ, DIM = 2048, 512
HEADS, HEAD_DIM = 16, 32
HALF = HEAD_DIM // 2
WINDOW = 256
TILES = SEQ // P
CHUNKS = DIM // P
GROUP = 512
GT = GROUP // P
GROUPS = SEQ // GROUP
PAIRS = TILES // 2
STEPS = HEADS * PAIRS
STACKED = 3 * HEAD_DIM
MAXROWS = 2
NSTACK = 3
ST_LAG = 10
PV_LAG = 11
NPT = 5
LN_EPS, RMS_EPS, THETA = 1e-5, 1e-6, 10000.0
SCALE = 1.0 / float(np.sqrt(HEAD_DIM))
TH_X, SC_X, TH_W, SC_W = 0.33, 0.5, 0.2, 0.6
LOWEST = -3.0e38


class Steps:

    def __init__(self, sem):
        self.sem = sem

    def done(self, instruction):
        return instruction.then_inc(self.sem, 1)

    def wait(self, engine, i):
        if i >= 0:
            engine.wait_ge(self.sem, i + 1)


class Arrivals:

    def __init__(self, sem, parts=1):
        self.sem, self.parts = sem, parts

    def sent(self, instruction):
        return instruction.then_inc(self.sem, 16)

    def wait(self, engine, use):
        if use >= 0:
            engine.wait_ge(self.sem, 16 * self.parts * (use + 1))


def build(nc, x_d, wqkv_d, qkw_d, wo_d, wf_d, rram_d, cos_d, sin_d, ident_d, out_d):
    ctx = ExitStack()
    with ctx:
        def sb(name, shape, dt=F32):
            return ctx.enter_context(nc.sbuf_tensor(name, shape, dt))

        def steps(name):
            return Steps(ctx.enter_context(nc.semaphore(name)))

        def arrivals(name, parts=1):
            return Arrivals(ctx.enter_context(nc.semaphore(name)), parts)

        sum_scr = nc.dram_tensor("sum_scr", [2, HEADS, SEQ // 2], F32, kind="Internal").ap()
        rec_scr = nc.dram_tensor("rec_scr", [2, HEADS, SEQ // 2], F32, kind="Internal").ap()
        qk_scr = nc.dram_tensor("qk_scr", [2, HEADS, 3, HEAD_DIM, SEQ], F32, kind="Internal").ap()
        zero_scr = nc.dram_tensor("zero_scr", [P - STACKED, SEQ], F32, kind="Internal").ap()
        ones_scr = nc.dram_tensor("ones_scr", [P - STACKED, SEQ], F32, kind="Internal").ap()

        region_w = sb("region_w", [P, 12288], F32R)
        wqk = region_w[:, 0:8192].rearrange("p (s k n) -> p s k n", s=2, k=CHUNKS)
        wv = region_w[:, 8192:12288].rearrange("p (s k n) -> p s k n", s=2, k=CHUNKS)
        q_stack = [region_w[:, 4096 * i:4096 * i + SEQ] for i in range(NSTACK)]
        k_stack = [region_w[:, 4096 * i + SEQ:4096 * i + 2 * SEQ] for i in range(NSTACK)]
        o_split = [region_w[:, 4096 * i:4096 * (i + 1)].rearrange("p (s c t) -> p s c t", s=2, c=CHUNKS)
                   for i in ((HEADS - 3) % NSTACK, (HEADS - 2) % NSTACK)]
        xq_t = [region_w[:, 512 * i:512 * (i + 1)].rearrange("p (c t) -> p c t", c=CHUNKS)
                for i in range(2)]

        region_t = sb("region_t", [P, 8192], F32R)
        x_t = [region_t[:, 4096 * i:4096 * (i + 1)].rearrange("p (s k t) -> p s k t", s=2, k=CHUNKS)
               for i in range(2)]
        wo = region_t[:, 0:4096].rearrange("p (s k n) -> p s k n", s=2, k=CHUNKS)
        wf = region_t[:, 4096:8192].rearrange("p (s k n) -> p s k n", s=2, k=CHUNKS)

        region_o = sb("region_o", [P, 8192])
        rope = region_o[:, 0:2048].rearrange("p (i t) -> p i t", i=4)
        unit = region_o[:, 2048:6144].rearrange("p (i t) -> p i t", i=8)
        square = region_o[:, 6144:7168].rearrange("p (i t) -> p i t", i=2)
        sqsum = region_o[:, 7168:8192].rearrange("p (i t) -> p i t", i=2)
        o_t = region_o[:, :].rearrange("p (c t) -> p c t", c=CHUNKS)

        v = sb("v", [P, TILES, DIM])
        x1 = v[:, 0:8, :]
        y3 = v[:, 8:10, :]
        below = v[:, 10, :].bitcast(BF16).rearrange("p (i n) -> p i n", i=2)
        xq = v[:, 11:14, :].rearrange("p i n -> p (i n)").bitcast(BF16).rearrange("p (i n) -> p i n", i=6)
        region_m = sb("region_m", [P, 5120])
        x_in = region_m[:, 0:2048].rearrange("p (i n) -> p i n", i=GT)
        x_hat = region_m[:, 2048:3072].rearrange("p (i n) -> p i n", i=2)
        trig = region_m[:, 3072:5120].rearrange("p (i s t) -> p i s t", i=2, s=2)
        prob = region_m[:, 0:768 * NPT].rearrange("p (i e t) -> p i e t", i=NPT, e=2)
        x3 = region_m[:, 0:2048].rearrange("p (i n) -> p i n", i=4)

        normed = sb("normed", [P, 4, GROUP])
        o_stage = normed[:, 2:4, :]
        out_stage = normed
        half_h = sb("half_h", [P, 4, GROUP], F32R)
        last_h = region_t[:, 0:2048].rearrange("p (i t) -> p i t", i=4)
        stage_w = sb("stage_w", [P, 2, 1024])
        v_raw = stage_w[:, :, :].rearrange("p i (a n) -> p (i a) n", a=2)
        rec_bc = sb("rec_bc", [P, SEQ])
        last_n = rec_bc[:, :].rearrange("p (i t) -> p i t", i=4)
        diag = sb("diag", [P, 2, GROUP])
        ident = sb("ident", [P, P])
        ident_bf = sb("ident_bf", [P, P], BF16)
        ones = sb("ones", [P, P])
        mask = sb("mask", [P, 2, P])
        qkw = sb("qkw", [P, 8])
        ln_bias = sb("ln_bias", [P, 2])
        stats = sb("stats", [P, GT, 6])
        mean_var = sb("mean_var", [P, GT, 2])
        dev = sb("dev", [P, GT])
        rstd = sb("rstd", [P, GT])
        rms_dev = sb("rms_dev", [P, 2, GT])
        rms_rec = sb("rms_rec", [P, 2, GT])
        exp_ready = sb("exp_ready", [P, 1])
        neg_max = sb("neg_max", [P, 2, TILES])
        max_split = sb("max_split", [P, 2, 2 * PAIRS], F32R)
        max_rows = sb("max_rows", [2 * PAIRS, 2, P], F32R)
        w_fold = region_m[:, 4096:5120].rearrange("p (i n) -> p i n", i=2)
        sums = sb("sums", [P, 2, 32])
        recs = sb("recs", [P, 2, 32])

        psum = ctx.enter_context(nc.psum_tensor("psum", [P, 8, 512], F32))
        BANK_XT, BANK_SUMS, BANK_PAIR, BANK_RMS = 0, 1, 2, 6
        BANK_ST, BANK_O = 4, 6
        BANK_WO, BANK_XQ, BANK_FFN = 0, 7, 5

        NWO = 5

        zero_set, a_zero = steps("zero_set"), arrivals("a_zero", 3)
        const_set, mask_set, ident_cast = steps("const_set"), steps("mask_set"), steps("ident_cast")
        a_const, a_qkw = arrivals("a_const"), arrivals("a_qkw")
        a_wqk = [arrivals(f"a_wqk{p}") for p in range(4)]
        a_wv = arrivals("a_wv")
        wv_high, wv_low = steps("wv_high"), steps("wv_low")
        a_x = arrivals("a_x", GT)
        a_trig = [arrivals(f"a_trig{i}", 2) for i in range(2)]
        a_half = [arrivals(f"a_half{i}", 3) for i in range(4)]
        a_last = [arrivals(f"a_last{i}", 3) for i in range(4)]
        w_high, w_low = steps("w_high"), steps("w_low")
        bn, aggr, ln_dev, ln_rstd, xhat = (steps(n) for n in ("bn", "aggr", "ln_dev", "ln_rstd", "xhat"))
        xtr, xt_high, xt_low = steps("xtr"), steps("xt_high"), steps("xt_low")
        qk_mm, v_mm, v_out = steps("qk_mm"), steps("v_mm"), steps("v_out")
        roped, squared, rotated, sq_added = steps("roped"), steps("squared"), steps("rotated"), steps("sq_added")
        sq_mm, r_dev, r_rec, diag_s, rms_mm = (steps(n) for n in ("sq_mm", "r_dev", "r_rec", "diag_s", "rms_mm"))
        scaled, q_high, q_low, k_low = steps("scaled"), steps("q_high"), steps("q_low"), steps("k_low")

        a_stack = [[arrivals(f"a_stack{i}{half}", 2) for half in range(2)] for i in range(NSTACK)]
        a_ones = [arrivals(f"a_ones{i}", 2) for i in range(NSTACK)]
        a_zeros = [[arrivals(f"a_zeros{i}{half}") for half in range(2)] for i in range(NSTACK)]
        a_rows = [arrivals(f"a_rows{i}") for i in range(2)]
        a_stage = [arrivals(f"a_stage{i}", 3) for i in range(2)]
        a_sums, a_recs, a_bc = arrivals("a_sums"), arrivals("a_recs"), arrivals("a_bc")
        a_wraw = [arrivals(f"a_wraw{i}") for i in range(2)]
        a_wraw2 = [arrivals(f"a_wraw2{i}", 2) for i in range(2)]
        filled, score, merged, maxed = (steps(n) for n in ("filled", "score", "merged", "maxed"))
        m_high, m_low, m_tr, m_row = steps("m_high"), steps("m_low"), steps("m_tr"), steps("m_row")
        st, expd, selected, pv, staged = (steps(n) for n in ("st", "expd", "selected", "pv", "staged"))
        recd, o_done = steps("recd"), steps("o_done")
        wo_high, wo_low = steps("wo_high"), steps("wo_low")
        w_tern, w_tr, wf_high, wf_low = steps("w_tern"), steps("w_tr"), steps("wf_high"), steps("wf_low")

        a_x3 = [arrivals(f"a_x3{i}") for i in range(4)]
        a_out = [arrivals(f"a_out{i}") for i in range(4)]
        o_low_dve = steps("o_low_dve")
        o_high, o_low, wo_mm, x1_s = steps("o_high"), steps("o_low"), steps("wo_mm"), steps("x1_s")
        bn3, aggr3, dev3, rstd3, y_s, below_s, xq_s = (
            steps(n) for n in ("bn3", "aggr3", "dev3", "rstd3", "y_s", "below_s", "xq_s"))
        xq_tr, xq_out, ffn_mm, out_s = steps("xq_tr"), steps("xq_out"), steps("ffn_mm"), steps("out_s")

        def f32(ap):
            return ap.bitcast(F32)

        x_tiles = x_d.rearrange("(t p) n -> t p n", p=P)
        out_tiles = out_d.rearrange("(t p) n -> t p n", p=P)

        def pair_free(engine, n):
            if n < 2:
                return
            g, p = divmod(n - 2, 6)
            if p < 4:
                roped.wait(engine, 4 * (4 * g + p) + 3)
                squared.wait(engine, 8 * g + 2 * p + 1)
            else:
                v_out.wait(engine, 4 * g + 2 * (p - 4) + 1)

        def qk_raw(p):
            if p < 2:
                return region_o[:, 1024 * p:1024 * (p + 1)].rearrange("p (k n) -> p k n", k=CHUNKS)
            return normed[:, 2 * p - 4:2 * p - 2, :].rearrange("p i (a n) -> p (i a) n", a=2)

        def w_halves(p):
            for half in range(2):
                yield (qk_raw(p).rearrange(
                           "c k (h x f) -> c x k h f", x=2, f=HALF)[:, half],
                       lambda s, half=half: wqk[:, s, :, 256 * p + P * half:256 * p + P * (half + 1)].rearrange(
                           "c k (h f) -> c k h f", f=HALF))

        def xt_bank(t):
            return (BANK_XT, BANK_RMS, BANK_RMS + 1, BANK_SUMS)[t] if t < GT else BANK_XT

        def high_buffer(n):
            return half_h[:, n % 4, :] if n < 8 * GROUPS - 4 else last_h[:, n % 4, :]

        def low_buffer(n):
            return normed[:, n % 4, :].bitcast(F32R) if n < 8 * GROUPS - 4 else last_n[:, n % 4, :].bitcast(F32R)

        def buffer_free(engine, n):
            if n < 8 * GROUPS - 4:
                a_half[n % 4].wait(engine, n // 4 - 1)

        def low_wait(engine, n):
            if n in LOW_DVE:
                k_low.wait(engine, LOW_DVE.index(n))
            else:
                q_low.wait(engine, n - sum(m < n for m in LOW_DVE))

        def half_from(h):
            return SEQ - GROUP if h == 0 else SEQ // 2

        def head_pair(n):
            return divmod(n, PAIRS)

        LOW_DVE = [8 * GROUPS - i for i in (8, 7, 4, 3)]

        M_TR = {4 * c + 5: c for c in range(2 * HEADS)}
        TERN = [36, 52, 68, 84]
        TERN_OPS = {t + 2 * i: (k, i) for k, t in enumerate(TERN) for i in range(4)}
        W_TR = {TERN[i // 2] + 8 + 6 * (i % 2): i for i in range(8)}
        STAGED = {4 * c + 5 + PV_LAG + 3 * (c == 0): c for c in range(2 * HEADS)}
        after = {2 * c + half: 32 * c + 29 + PV_LAG + 6 * half for c in range(CHUNKS) for half in range(2)}
        LOAD_SUMS = {n + 2: u for u, n in after.items()}
        RECIP = {n + 5 + 2 * (u % 2): u for u, n in after.items()}
        SPREAD = {n + 7 + 2 * (u % 2): u for u, n in after.items()}
        DIVIDE = {n + 10 + 3 * (u % 2) + 2 * q: 2 * u + q for u, n in after.items() for q in range(2)}
        EARLY_O = [STEPS - 3, STEPS + 1, STEPS + 5]
        SPLIT_O = [(0, 0), (0, 1), (0, 2), (1, 0), (1, 1), (1, 2), (0, 3), (1, 3)] + [
            (g, c) for g in (2, 3) for c in range(CHUNKS)]
        BY_DVE = (0, CHUNKS - 1)
        LATE_STORES = {6: 2, 12: 3, 18: 6, 22: 7}
        LAST = STEPS + 32
        WO_S = [16, 20, 24, 28]

        block = ctx.enter_context(nc.Block())

        @block.sync
        def _(eng):
            def load_x(g):
                for i in range(GT):
                    a_x.sent(eng.dma_start(x_in[:, i, :], x_tiles[GT * g + i]))

            def load_wo(k):
                if k >= 2:
                    wo_low.wait(eng, k - 2)
                a_wraw[k % 2].sent(eng.dma_start(stage_w[:, k % 2, 0:DIM], wo_d[P * k:P * (k + 1), :]))

            def load_trig(g):
                cols = slice(GROUP * g, GROUP * (g + 1))
                a_trig[g % 2].sent(eng.dma_start(trig[:, g % 2, 0, :], cos_d[:, cols]))
                a_trig[g % 2].sent(eng.dma_start(trig[:, g % 2, 1, :], sin_d[:, cols]))

            def store_half(g, c):
                n = 8 * g + c
                qk, hg, half = c // 4, (c // 2) % 2, c % 2
                for s in range(3):
                    high = s != (1 if qk else 2)
                    if s == 0:
                        q_high.wait(eng, n)
                        low_wait(eng, n)
                    dst = qk_scr[qk, 8 * hg:8 * hg + 8, s, HALF * half:HALF * (half + 1),
                                 GROUP * g:GROUP * (g + 1)]
                    stored = a_half if n < 8 * GROUPS - 4 else a_last
                    stored[n % 4].sent(eng.dma_start(dst, f32(high_buffer(n) if high else low_buffer(n))))

            load_x(0)
            a_const.sent(eng.dma_start(ident[:, :], ident_d))
            w_rows = wqkv_d.rearrange("(k p) n -> p k n", p=P)
            for p in range(4):
                cols = slice(256 * p, 256 * (p + 1))
                a_wqk[p].sent(eng.dma_start(qk_raw(p), w_rows[:, :, cols]))
            a_qkw.sent(eng.dma_start(qkw[:, :], qkw_d))
            load_trig(0)
            a_wv.sent(eng.dma_start(v_raw, w_rows[:, :, 2 * DIM:3 * DIM]))
            zero_set.wait(eng, 0)
            rest = P - STACKED
            a_zero.sent(eng.dma_start(zero_scr, rec_bc[0:rest, :]))
            a_zero.sent(eng.dma_start(ones_scr[MAXROWS:rest, :], rec_bc[0:rest - MAXROWS, :]))
            const_set.wait(eng, 3)
            a_zero.sent(eng.dma_start(ones_scr[0:MAXROWS, :].rearrange("r (b t) -> (r b) t", t=P),
                                      ones[0:MAXROWS * SEQ // P, :]))
            xhat.wait(eng, GT - 1)
            load_x(1)
            for g in range(GROUPS):
                if g == 1:
                    wv_low.wait(eng, CHUNKS - 1)
                    for k in range(2):
                        load_wo(k)
                if g + 1 < GROUPS:
                    roped.wait(eng, 16 * (g - 1) + 15)
                    load_trig(g + 1)
                if g:
                    for c in range(4, 8):
                        store_half(g - 1, c)
                if g + 2 < GROUPS:
                    xhat.wait(eng, GT * (g + 1) + 3)
                    load_x(g + 2)
                if g + 1 < GROUPS:
                    for c in range(4):
                        store_half(g, c)

            def prepare_stack(i):
                a_zero.wait(eng, 0)
                if i < 2:
                    qk_mm.wait(eng, 8 * GROUPS - 1)
                else:
                    v_mm.wait(eng, TILES - 1)
                a_ones[i].sent(eng.dma_start(f32(q_stack[i][STACKED:P, :]), zero_scr))
                a_ones[i].sent(eng.dma_start(f32(k_stack[i][STACKED:P, :]), ones_scr))

            def load_stack(h, half):
                i = h % NSTACK
                cols = slice(half_from(h), SEQ) if half else slice(0, half_from(h))
                if h >= NSTACK:
                    st.wait(eng, TILES * (h - NSTACK) + TILES // 2 * (half + 1) - 1)
                    a_zeros[i][half].sent(eng.dma_start(f32(q_stack[i][STACKED:STACKED + MAXROWS, cols]),
                                                        zero_scr[0:MAXROWS, cols]))
                for qk, stack in ((0, q_stack), (1, k_stack)):
                    a_stack[i][half].sent(eng.dma_start(f32(stack[i][0:STACKED, cols]),
                                                        qk_scr[qk, h].rearrange("s d t -> (s d) t")[:, cols]))

            for i in range(2):
                a_half[i].wait(eng, 2 * (GROUPS - 1) - 1)
            for i in range(2):
                prepare_stack(i)
            load_stack(0, 0)
            for c in (0, 1, 4, 5):
                store_half(GROUPS - 1, c)
            for i in range(2):
                a_half[i].wait(eng, 2 * GROUPS - 2)
                a_last[i].wait(eng, 0)
            load_stack(0, 1)
            load_stack(1, 0)
            def load_x3(t):
                if t >= 4:
                    x1_s.wait(eng, t - 4)
                a_x3[t % 4].sent(eng.dma_start(x3[:, t % 4, :], x_tiles[t]))

            for s in range(LAST):
                if s in M_TR:
                    c = M_TR[s]
                    h, half = divmod(c, 2)
                    m_row.wait(eng, c)
                    dst = q_stack[h % NSTACK][STACKED:STACKED + MAXROWS, 1024 * half:1024 * (half + 1)]
                    a_rows[c % 2].sent(eng.dma_start(f32(dst), f32(max_rows[:, c % 2, :])))
                if s == 6:
                    load_stack(1, 1)
                if s == 9:
                    prepare_stack(2)
                if s in (9, 10):
                    load_stack(2, s - 9)
                if s in LATE_STORES:
                    store_half(GROUPS - 1, LATE_STORES[s])
                if s == 30:
                    for i in range(2, 4):
                        a_half[i].wait(eng, 2 * GROUPS - 2)
                        a_last[i].wait(eng, 0)
                if s % PAIRS == 6 and NSTACK <= s // PAIRS + 2 < HEADS:
                    load_stack(s // PAIRS + 2, 0)
                if s % PAIRS == 2 and NSTACK <= s // PAIRS + 1 < HEADS:
                    load_stack(s // PAIRS + 1, 1)
                if s in STAGED:
                    c = STAGED[s]
                    h, half = divmod(c, 2)
                    staged.wait(eng, c)
                    tokens = slice(1024 * half, 1024 * (half + 1))
                    rows = HEAD_DIM * (h % 4)
                    dst = sum_scr[half, h, :].rearrange("(j e t) -> e j t", e=2, t=2 * P)
                    src = o_stage[HEAD_DIM:HEAD_DIM + 65:64, c % 2, :].rearrange("p (j t) -> p j t", t=2 * P)
                    a_stage[c % 2].sent(eng.dma_start(dst, src))
                    for e in range(2):
                        dst = o_t[rows:rows + HEAD_DIM, h // 4, tokens].rearrange("p (j e t) -> p e j t", e=2, t=2 * P)
                        src = o_stage[64 * e:64 * e + HEAD_DIM, c % 2, :].rearrange("p (j t) -> p j t", t=2 * P)
                        a_stage[c % 2].sent(eng.dma_start(dst[:, e], src))
                if s in SPREAD:
                    u = SPREAD[s]
                    c, half = divmod(u, 2)
                    a_recs.wait(eng, u)
                    o_done.wait(eng, 2 * (u - 2) + 1)
                    a_bc.sent(eng.dma_start(
                        rec_bc[:, 1024 * half:1024 * (half + 1)],
                        rec_scr[half, 4 * c:4 * c + 4, :].rearrange("h (o t) -> h o t", o=1).to_broadcast(
                            [4, HEAD_DIM, SEQ // 2])))
                if s in LOAD_SUMS:
                    u = LOAD_SUMS[s]
                    c, half = divmod(u, 2)
                    a_stage[half].wait(eng, 4 * c + 3)
                    recd.wait(eng, u - 2)
                    a_sums.sent(eng.dma_start(sums[:, u % 2, :], sum_scr[half, 4 * c:4 * c + 4, :].rearrange(
                        "h (i t) -> (h i) t", t=32)))
                if s in RECIP:
                    u = RECIP[s]
                    c, half = divmod(u, 2)
                    recd.wait(eng, u)
                    a_recs.sent(eng.dma_start(rec_scr[half, 4 * c:4 * c + 4, :].rearrange("h (i t) -> (h i) t", t=32),
                                              recs[:, u % 2, :]))
                if s in (STEPS + PV_LAG + 2, STEPS + PV_LAG + 4):
                    expd.wait(eng, 2 * STEPS - 1)
                    selected.wait(eng, 2 * STEPS - HEADS - 1)
                    pv.wait(eng, STEPS // 2 - 1)
                    for t in ((0, 1) if s == STEPS + PV_LAG + 2 else (2, 3)):
                        load_x3(t)
                if s + 6 in WO_S[2:]:
                    load_wo(WO_S.index(s + 6))
                if s + 8 in TERN:
                    k = TERN.index(s + 8)
                    if k == 0:
                        wo_low.wait(eng, 3)
                    if k >= 2:
                        w_tern.wait(eng, 4 * (k - 2) + 3)
                    a_wraw2[k % 2].sent(eng.dma_start(stage_w[:, k % 2, 0:DIM], wf_d[P * k:P * (k + 1), :]))
                    a_wraw2[k % 2].sent(eng.dma_start(stage_w[:, k % 2, DIM:2 * DIM], rram_d[P * k:P * (k + 1), :]))

            for t in range(TILES):
                if t + 4 < TILES:
                    load_x3(t + 4)
                if t >= 3:
                    out_s.wait(eng, t - 3)
                    a_out[(t - 3) % 4].sent(eng.dma_start(out_tiles[t - 3], out_stage[:, (t - 3) % 4, :]))
            for t in range(TILES - 3, TILES):
                out_s.wait(eng, t)
                a_out[t % 4].sent(eng.dma_start(out_tiles[t], out_stage[:, t % 4, :]))
            for i in range(4):
                a_out[i].wait(eng, TILES // 4 - 1)

        @block.tensor
        def _(eng):
            SPLIT = ((0, 0), (0, 1), (1, 0))

            def transpose_x(t):
                xhat.wait(eng, t)
                if t >= GT:
                    xt_high.wait(eng, t - 1)
                    xt_low.wait(eng, t - 1)
                for k in range(CHUNKS):
                    last = nc.tensor.transpose(psum[:, xt_bank(t), P * k:P * (k + 1)],
                                               x_hat[:, t % 2, P * k:P * (k + 1)], ident[:, :])
                xtr.done(last)

            def project_qk(g, p):
                n = 6 * g + p
                pair_free(eng, n)
                for half in range(2):
                    if g == 0:
                        w_high.wait(eng, 2 * p + half)
                        w_low.wait(eng, 2 * p + half)
                    for k in range(CHUNKS):
                        for a, b in SPLIT:
                            w = wqk[:, a, k, 256 * p + P * half:256 * p + P * (half + 1)]
                            last = nc.tensor.matmul(psum[:, BANK_PAIR + 2 * (n % 2) + half, :], w,
                                                    x_t[g % 2][:, b, k, :], start=(k == 0 and a + b == 0),
                                                    stop=(k == CHUNKS - 1 and a == 1))
                    qk_mm.done(last)

            def project_v(g, p, e):
                n, i = 6 * g + 4 + p, 2 * p + e
                pair_free(eng, n)
                if g == 0:
                    wv_high.wait(eng, CHUNKS - 1)
                    wv_low.wait(eng, CHUNKS - 1)
                j = 0
                for k in range(CHUNKS):
                    for a, b in SPLIT:
                        last = nc.tensor.matmul(psum[:, BANK_PAIR + 2 * (n % 2) + e, :],
                                                x_t[g % 2][:, b, k, P * i:P * (i + 1)],
                                                wv[:, a, k, :], start=(j == 0), stop=(j == 11))
                        j += 1
                v_mm.done(last)

            def sum_squares(g, s):
                sq_added.wait(eng, 6 * g + 3 * s + 2)
                r_dev.wait(eng, 2 * g + s - 1)
                for i in range(GT):
                    last = nc.tensor.matmul(psum[:, BANK_SUMS, i:i + 1], sqsum[:, s, P * i:P * (i + 1)],
                                            ones[:, 0:1], start=True, stop=True)
                sq_mm.done(last)

            def spread_rms(g, s):
                diag_s.wait(eng, GT * (2 * g + s) + GT - 1)
                if g:
                    scaled.wait(eng, 8 * (g - 1) + 4 * s + 3)
                rms_mm.done(nc.tensor.matmul(psum[:, BANK_RMS + s, :], ones[:, :], diag[:, s, :],
                                             start=True, stop=True))

            a_const.wait(eng, 0)
            const_set.wait(eng, 3)
            for t in range(GT):
                transpose_x(t)
            for g in range(GROUPS):
                xt_high.wait(eng, GT * g + 3)
                xt_low.wait(eng, GT * g + 3)
                for p in range(4):
                    project_qk(g, p)
                    if p == 2:
                        sum_squares(g, 0)
                    if g + 1 < GROUPS:
                        transpose_x(GT * (g + 1) + p)
                spread_rms(g, 0)
                for e in range(2):
                    project_v(g, 0, e)
                sum_squares(g, 1)
                for e in range(2):
                    project_v(g, 1, e)
                    if e == (1 if g + 1 < GROUPS else 0):
                        spread_rms(g, 1)

            def scores(n):
                h, j = head_pair(n)
                if j == 0:
                    filled.wait(eng, h)
                    a_ones[h % NSTACK].wait(eng, 0)
                if j in (0, half_from(h) // (2 * P)):
                    half = int(j > 0)
                    a_stack[h % NSTACK][half].wait(eng, h // NSTACK)
                    a_zeros[h % NSTACK][half].wait(eng, h // NSTACK - 1)
                if n >= 2:
                    maxed.wait(eng, n - 2)
                elif n == 0:
                    r_dev.wait(eng, 2 * GROUPS - 1)
                    xt_low.wait(eng, TILES - 1)
                else:
                    v_out.wait(eng, TILES - 3)
                qs, ks = q_stack[h % NSTACK], k_stack[h % NSTACK]
                for e in range(2):
                    qt = 2 * j + e
                    k0 = max(0, qt - 2)
                    last = nc.tensor.matmul(psum[:, 2 * (n % 2) + e, P * (k0 - qt + 2):3 * P],
                                            qs[:, P * qt:P * (qt + 1)],
                                            ks[:, P * k0:P * (qt + 1)], start=True, stop=True)
                score.done(last)

            def maxima_to_rows(c, s):
                m_low.wait(eng, c)
                m_tr.done(nc.tensor.transpose(psum[0:2 * PAIRS, 2 * (s % 2), 3 * P:4 * P],
                                              f32(max_split[:, c % 2, :]), ident[:, :]))

            def transpose_w(i):
                k, d0 = divmod(i, 2)
                w_tern.wait(eng, 4 * k + 3)
                return k, 2 * d0

            def scores_t(n):
                h, j = head_pair(n)
                c = 2 * h + min(2 * j + 3, TILES - 1) // PAIRS
                a_rows[c % 2].wait(eng, c // 2)
                if n == 0:
                    v_out.wait(eng, TILES - 1)
                qs, ks = q_stack[h % NSTACK], k_stack[h % NSTACK]
                for e in range(2):
                    kt = 2 * j + e
                    expd.wait(eng, 2 * (n - 1) + e)
                    q1 = min(TILES, kt + 3)
                    last = nc.tensor.matmul(psum[:, BANK_ST + e, 0:P * (q1 - kt)],
                                            ks[:, P * kt:P * (kt + 1)],
                                            qs[:, P * kt:P * q1], start=True, stop=True)
                    st.done(last)

            def products_of(jj):
                if jj == 0:
                    return [(0, 0, 1, True, True), (0, 1, 1, True, False), (1, 1, 1, False, True)]
                return [(2 * jj - 1, 2 * jj, 2, True, False), (2 * jj - 2, 2 * jj, 1, False, False),
                        (2 * jj + 1, 2 * jj + 1, 1, False, False), (2 * jj, 2 * jj, 2, False, True)]

            def times_v(n, part):
                h, j = head_pair(n)
                c = n // 4
                selected.wait(eng, (2 * PAIRS - 1) * h + min(2 * (j - 1 + part) + 1, 2 * PAIRS - 2))
                if n % 4 == 1 and part == 0:
                    staged.wait(eng, c - 2)
                    if n == 1:
                        scaled.wait(eng, 8 * GROUPS - 1)
                first = 2 * P * (n // 2 % 2)
                lanes = [products_of(j - 1), products_of(j)]
                for i in (2 * part, 2 * part + 1):
                    for lane in range(2):
                        if i >= len(lanes[lane]):
                            continue
                        kt, q0, width, start, stop = lanes[lane][i]
                        probs = prob[:, (n - j + kt // 2) % NPT, kt % 2, P * (q0 - kt):P * (q0 - kt + width)]
                        at = first + P * (q0 - 2 * (j - 1 + lane))
                        for r, w in ((2 * lane, v[:, kt, HEAD_DIM * h:HEAD_DIM * (h + 1)]),
                                     (2 * lane + 1, ones[:, 0:HEAD_DIM])):
                            last = nc.tensor.matmul(psum[32 * r:32 * r + 32, BANK_O + c % 2, at:at + P * width], w,
                                                    probs, start=start, stop=stop, tile_position=(0, 32 * r))
                if part:
                    pv.done(last)

            for s in range(STEPS + PV_LAG + 1):
                if 0 <= s - ST_LAG < STEPS:
                    scores_t(s - ST_LAG)
                if s < STEPS:
                    scores(s)
                else:
                    if s - 2 < STEPS:
                        maxed.wait(eng, s - 2)
                if s in M_TR:
                    maxima_to_rows(M_TR[s], s)
                if s in W_TR:
                    k, d0 = transpose_w(W_TR[s])
                    for e in range(2):
                        last = nc.tensor.transpose(psum[:, 2 * (s % 2) + e, 3 * P:4 * P],
                                                   w_fold[:, k % 2, P * (d0 + e):P * (d0 + e + 1)], ident[:, :])
                    w_tr.done(last)
                n = s - PV_LAG
                if n > 0:
                    times_v(n - 1 + n % 2, 1 - n % 2)

            def project_o(t, chunks):
                g, i = divmod(t, GT)
                if chunks[0] == 0:
                    if t >= NWO:
                        x1_s.wait(eng, t - NWO)
                    elif t == 0:
                        wo_high.wait(eng, CHUNKS - 1)
                        wo_low.wait(eng, CHUNKS - 1)
                        maxed.wait(eng, STEPS - 1)
                        expd.wait(eng, 2 * STEPS - 1)
                for c in chunks:
                    n = SPLIT_O.index((g, c))
                    o_high.wait(eng, n)
                    if (g, c) == BY_DVE:
                        o_low_dve.wait(eng, 0)
                    else:
                        o_low.wait(eng, n - (n > SPLIT_O.index(BY_DVE)))
                    for a, b in SPLIT:
                        last = nc.tensor.matmul(psum[:, BANK_WO + t % NWO, :],
                                                o_split[g % 2][:, a, c, P * i:P * (i + 1)], wo[:, b, c, :],
                                                start=(c == 0 and a + b == 0), stop=(c == CHUNKS - 1 and a == 1))
                if chunks[-1] == CHUNKS - 1:
                    wo_mm.done(last)

            def transpose_xq(t):
                xq_s.wait(eng, t)
                xq_out.wait(eng, t - 1)
                if t == 0:
                    staged.wait(eng, 2 * HEADS - 1)
                for c in range(CHUNKS):
                    last = nc.tensor.transpose(psum[:, BANK_XQ, 0:DIM // 2].bitcast(BF16)[:, P * c:P * (c + 1)],
                                               xq[:, t % 6, P * c:P * (c + 1)], ident_bf[:, :])
                xq_tr.done(last)

            def ffn(t):
                xq_out.wait(eng, t)
                if t == 0:
                    wf_low.wait(eng, 15)
                if t >= 2:
                    out_s.wait(eng, t - 2)
                else:
                    expd.wait(eng, 2 * STEPS - 1)
                j = 0
                for c in range(CHUNKS):
                    for a in range(2):
                        last = nc.tensor.matmul(psum[:, BANK_FFN + t % 2, :], xq_t[t % 2][:, c, :], wf[:, a, c, :],
                                                start=(j == 0), stop=(j == 7))
                        j += 1
                ffn_mm.done(last)

            m_row.wait(eng, 2 * HEADS - 1)
            for t in range(NWO):
                project_o(t, range(CHUNKS - 1))
            for t in range(TILES + 6):
                if t < TILES:
                    project_o(t, range(CHUNKS - 1 if t < NWO else 0, CHUNKS))
                if 0 <= t - 5 < TILES:
                    transpose_xq(t - 5)
                if 0 <= t - 6 < TILES:
                    ffn(t - 6)

        @block.scalar
        def _(eng):
            const_set.wait(eng, 3)

            def ln_sqrt(g):
                aggr.wait(eng, GT * g + 3)
                ln_rstd.wait(eng, g - 1)
                ln_dev.done(nc.scalar.activation(dev[:, :], mean_var[:, :, 1], ACT.Sqrt, bias=ln_bias[:, 0:1]))

            def high_x(t):
                xtr.wait(eng, t)
                g, i = divmod(t, GT)
                if g >= 2:
                    v_mm.wait(eng, GT * (g - 2) + 3)
                xt_high.done(nc.scalar.copy(x_t[g % 2][:, 0, :, P * i:P * (i + 1)],
                                            psum[:, xt_bank(t), :].rearrange("p (k t) -> p k t", k=CHUNKS)))

            def squares(g, p):
                for half in range(2):
                    c = 2 * p + half
                    qk_mm.wait(eng, 8 * g + c)
                    m = 4 * g + p - 1
                    if m >= 0:
                        sq_added.wait(eng, 3 * (m // 2) + (0 if m % 2 == 0 else 2))
                    squared.done(nc.scalar.activation(square[:, half, :],
                                                      psum[:, BANK_PAIR + 2 * ((6 * g + p) % 2) + half, :],
                                                      ACT.Square))

            def rms_sqrt(g, s):
                m = 2 * g + s
                sq_mm.wait(eng, m)
                if g:
                    r_rec.wait(eng, m - 2)
                r_dev.done(nc.scalar.activation(rms_dev[:, s, :], psum[:, BANK_SUMS, 0:GT], ACT.Sqrt,
                                                bias=ln_bias[:, 1:2], scale=1.0 / DIM))

            def evacuate_v(g, p, e):
                t = GT * g + 2 * p + e
                v_mm.wait(eng, t)
                v_out.done(nc.scalar.copy(v[:, t, :], psum[:, BANK_PAIR + 2 * ((6 * g + 4 + p) % 2) + e, :]))

            def high_qk(g, c):
                n = 8 * g + c
                scaled.wait(eng, n)
                buffer_free(eng, n)
                q_high.done(nc.scalar.copy(high_buffer(n), f32(low_buffer(n))))

            ln_sqrt(0)
            def high_w(p):
                a_wqk[p].wait(eng, 0)
                for raw, kept in w_halves(p):
                    w_high.done(nc.scalar.copy(kept(0), raw))

            high_w(0)
            for t in range(GT):
                high_x(t)
            high_w(1)
            for g in range(GROUPS):
                if g + 1 < GROUPS:
                    ln_sqrt(g + 1)
                for p in range(4):
                    squares(g, p)
                    if p == 2:
                        rms_sqrt(g, 0)
                    if g + 1 < GROUPS:
                        high_x(GT * (g + 1) + p)
                    if p < 2 and g:
                        high_qk(g - 1, 4 + 2 * p)
                        high_qk(g - 1, 5 + 2 * p)
                    if p < 2 and g == 0:
                        high_w(2 + p)
                    if p == 2 and g == 0:
                        a_wv.wait(eng, 0)
                        for k in range(CHUNKS):
                            wv_high.done(nc.scalar.copy(wv[:, 0, k, :], v_raw[:, k, :]))
                for e in range(2):
                    evacuate_v(g, 0, e)
                    if e:
                        rms_sqrt(g, 1)
                    high_qk(g, 2 * e)
                    high_qk(g, 2 * e + 1)
                for e in range(2):
                    evacuate_v(g, 1, e)
                    if g + 1 == GROUPS:
                        high_qk(g, 4 + 2 * e)
                        high_qk(g, 5 + 2 * e)

            nc.scalar.activation(exp_ready[:, :], ln_bias[:, 0:1], ACT.Exp)

            def exponentials(n):
                h, j = head_pair(n)
                pv.wait(eng, (n - NPT + 1) // 2)
                if n == 0:
                    xtr.wait(eng, TILES - 1)
                    roped.wait(eng, 16 * GROUPS - 1)
                for e in range(2):
                    st.wait(eng, 2 * n + e)
                    cols = P * min(3, TILES - 2 * j - e)
                    expd.done(nc.scalar.activation(prob[:, n % NPT, e, 0:cols], psum[:, BANK_ST + e, 0:cols],
                                                   ACT.Exp, scale=SCALE))

            def stage(c):
                pv.wait(eng, 2 * c + 1)
                if c >= 2:
                    a_stage[c % 2].wait(eng, c // 2 - 1)
                if c == 0:
                    for i in range(2, 4):
                        a_half[i].wait(eng, 2 * GROUPS - 2)
                staged.done(nc.scalar.copy(o_stage[:, c % 2, :], psum[:, BANK_O + c % 2, :]))

            def high_o(g, chunks):
                for c in chunks:
                    o_done.wait(eng, GROUPS * c + g)
                    if g < 2 and c == 0:
                        st.wait(eng, TILES * (HEADS - 2 + g) - 1)
                    if g >= 2:
                        wo_mm.wait(eng, GT * (g - 2) + 3)
                    o_high.done(nc.scalar.copy(o_split[g % 2][:, 0, c, :], o_t[:, c, GROUP * g:GROUP * (g + 1)]))

            for s in range(STEPS + PV_LAG + 3):
                at_end = s >= STEPS
                if s in STAGED and at_end:
                    stage(STAGED[s])
                if 0 <= s - ST_LAG < STEPS:
                    exponentials(s - ST_LAG)
                if s in STAGED and not at_end:
                    stage(STAGED[s])
                if s in EARLY_O:
                    high_o(0, [EARLY_O.index(s)])
                if s in WO_S:
                    k = WO_S.index(s)
                    a_wraw[k % 2].wait(eng, k // 2)
                    a_last[k].wait(eng, 0)
                    wo_high.done(nc.scalar.copy(wo[:, 0, k, :], stage_w[:, k % 2, 0:DIM]))

            high_o(1, range(CHUNKS - 1))
            high_o(0, [CHUNKS - 1])
            high_o(1, [CHUNKS - 1])
            copies = {u + 3 if u < 5 else u + 5: u for u in range(TILES)}
            splits = {1: (2, range(CHUNKS - 1)), 5: (2, [CHUNKS - 1]), 8: (3, range(CHUNKS))}
            for t in range(TILES + 5):
                if t in copies:
                    u = copies[t]
                    xq_tr.wait(eng, u)
                    ffn_mm.wait(eng, u - 2)
                    xq_out.done(nc.scalar.copy(
                        xq_t[u % 2][:, :, :],
                        psum[:, BANK_XQ, 0:DIM // 2].bitcast(BF16).rearrange("p (c t) -> p c t", c=CHUNKS)))
                if t in splits:
                    high_o(*splits[t])
                if t < TILES:
                    aggr3.wait(eng, t)
                    rstd3.wait(eng, t - 4)
                    dev3.done(nc.scalar.activation(dev[:, t % 4:t % 4 + 1], mean_var[:, t % 4, 1:2], ACT.Sqrt,
                                                   bias=ln_bias[:, 0:1]))

        @block.gpsimd
        def _(eng):
            const_set.done(nc.gpsimd.memset(ones[:, :], 1.0))
            const_set.done(nc.gpsimd.memset(ln_bias[:, 0:1], LN_EPS))
            const_set.done(nc.gpsimd.memset(ln_bias[:, 1:2], RMS_EPS))
            const_set.done(nc.gpsimd.memset(mask[:, :, :], 1.0))
            zero_set.done(nc.gpsimd.memset(rec_bc[:, :], 0.0))
            const_set.wait(eng, 3)
            mask_set.done(nc.gpsimd.affine_select(out=mask[:, :, :], in_=mask[:, :, :], compare_op=ALU.is_ge,
                                                  fill=0.0, base=0, pattern=[[0, 2], [-1, P]],
                                                  channel_multiplier=1))

            def rotate(g, p):
                m = 4 * g + p
                u = 4 * (p // 2) + 2 * (p % 2)
                if g:
                    scaled.wait(eng, 8 * (g - 1) + 2 * p + 1)
                roped.wait(eng, 4 * m + 1)
                rotated.done(nc.gpsimd.tensor_tensor(unit[:, u, :], rope[:, 0, :], rope[:, 1, :], ALU.subtract))
                roped.wait(eng, 4 * m + 3)
                rotated.done(nc.gpsimd.tensor_tensor(unit[:, u + 1, :], rope[:, 2, :], rope[:, 3, :], ALU.add))

            def add_squares(g, p):
                s = p // 2
                squared.wait(eng, 8 * g + 2 * p + 1)
                if p % 2 == 0:
                    if g:
                        sq_mm.wait(eng, 2 * (g - 1) + s)
                    sq_added.done(nc.gpsimd.tensor_tensor(sqsum[:, s, :], square[:, 0, :], square[:, 1, :], ALU.add))
                else:
                    for half in range(2):
                        n = 6 * g + 3 * s + 1 + half
                        sq_added.wait(eng, n - 1)
                        sq_added.done(nc.gpsimd.tensor_tensor(sqsum[:, s, :], sqsum[:, s, :], square[:, half, :],
                                                              ALU.add))

            def low_qk(g, c):
                n = 8 * g + c
                if n not in LOW_DVE:
                    q_high.wait(eng, n)
                    q_low.done(nc.gpsimd.tensor_tensor(low_buffer(n), f32(low_buffer(n)), f32(high_buffer(n)),
                                                       ALU.subtract))

            for g in range(GROUPS):
                for p in range(4):
                    add_squares(g, p)
                    rotate(g, p)
                    if p < 2 and g:
                        low_qk(g - 1, 4 + 2 * p)
                        low_qk(g - 1, 5 + 2 * p)
                for c in range(4):
                    low_qk(g, c)
            for c in range(4, 8):
                low_qk(GROUPS - 1, c)

            def low_o(g, c):
                o_high.wait(eng, SPLIT_O.index((g, c)))
                o_low.done(nc.gpsimd.tensor_tensor(o_split[g % 2][:, 1, c, :], o_t[:, c, GROUP * g:GROUP * (g + 1)],
                                                   f32(o_split[g % 2][:, 0, c, :]), ALU.subtract))

            for n in range(STEPS):
                if n + ST_LAG - 2 in EARLY_O:
                    low_o(0, EARLY_O.index(n + ST_LAG - 2))
                h, j = head_pair(n)
                expd.wait(eng, 2 * n + 1)
                near = prob[:, n % NPT, :, 0:P]
                selected.done(nc.gpsimd.affine_select(out=near, in_=near, compare_op=ALU.is_ge, fill=0.0, base=0,
                                                      pattern=[[0, 2], [1, P]], channel_multiplier=-1))
                if j < PAIRS - 1:
                    far = prob[:, n % NPT, :, 2 * P:3 * P]
                    selected.done(nc.gpsimd.affine_select(out=far, in_=far, compare_op=ALU.is_ge, fill=0.0,
                                                          base=WINDOW - 1 - 2 * P, pattern=[[0, 2], [-1, P]],
                                                          channel_multiplier=1))

            for g, c in SPLIT_O[CHUNKS - 1:]:
                if (g, c) == BY_DVE:
                    continue
                if (g, c) == (2, CHUNKS - 1):
                    a_bc.wait(eng, 2 * CHUNKS - 1)
                    for i in (2, 3):
                        o_done.wait(eng, GROUPS * CHUNKS - 5 + i)
                        cols = slice(GROUP * i, GROUP * (i + 1))
                        o_done.done(nc.gpsimd.tensor_tensor(o_t[:, CHUNKS - 1, cols], o_t[:, CHUNKS - 1, cols],
                                                            rec_bc[:, cols], ALU.mult))
                low_o(g, c)

        @block.vector
        def _(eng):
            vec = nc.vector

            def ln_stats(g):
                for i in range(GT):
                    a_x.wait(eng, g)
                    xhat.wait(eng, GT * (g - 1) + i)
                    bn.done(vec.bn_stats(stats[:, i, :], x_in[:, i, :]))
                for i in range(GT):
                    bn.wait(eng, GT * g + i)
                    aggr.done(vec.bn_aggr(mean_var[:, i, :], stats[:, i, :]))

            def ln_recip(g):
                ln_dev.wait(eng, g)
                ln_rstd.done(vec.reciprocal(rstd[:, :], dev[:, :]))

            def normalise(t):
                g, i = divmod(t, GT)
                ln_rstd.wait(eng, g)
                xtr.wait(eng, t - 2)
                xhat.done(vec.tensor_scalar(x_hat[:, t % 2, :], x_in[:, i, :], mean_var[:, i, 0:1],
                                            rstd[:, i:i + 1], ALU.subtract, ALU.mult))

            def low_x(t):
                g, i = divmod(t, GT)
                xt_high.wait(eng, t)
                xt_low.done(vec.tensor_tensor(x_t[g % 2][:, 1, :, P * i:P * (i + 1)],
                                              psum[:, xt_bank(t), :].rearrange("p (k t) -> p k t", k=CHUNKS),
                                              f32(x_t[g % 2][:, 0, :, P * i:P * (i + 1)]), ALU.subtract))

            def rope_products(g, p):
                m = 4 * g + p
                banks = BANK_PAIR + 2 * ((6 * g + p) % 2)
                squared.wait(eng, 8 * g + 2 * p + 1)
                a_trig[g % 2].wait(eng, g // 2)
                a_qkw.wait(eng, 0)
                for i, (half, s) in enumerate(((0, 0), (1, 1), (1, 0), (0, 1))):
                    if m:
                        rotated.wait(eng, 2 * (m - 1) + i // 2)
                    roped.done(vec.scalar_tensor_tensor(rope[:, i, :], psum[:, banks + half, :],
                                                        qkw[:, 2 * p + half:2 * p + half + 1],
                                                        trig[:, g % 2, s, :], ALU.mult, ALU.mult))

            def rms_recip(g, s):
                m = 2 * g + s
                r_dev.wait(eng, m)
                r_rec.done(vec.reciprocal(rms_rec[:, s, :], rms_dev[:, s, :]))
                r_rec.wait(eng, m)
                if g:
                    rms_mm.wait(eng, m - 2)
                for i in range(GT):
                    diag_s.done(vec.tensor_scalar(diag[:, s, P * i:P * (i + 1)], ident[:, :],
                                                  rms_rec[:, s, i:i + 1], None, ALU.mult))

            def scale_qk(g, c):
                n, s = 8 * g + c, c // 4
                rms_mm.wait(eng, 2 * g + s)
                rotated.wait(eng, n)
                buffer_free(eng, n)
                scaled.done(vec.tensor_tensor(f32(low_buffer(n)), unit[:, c, :], psum[:, BANK_RMS + s, :],
                                              ALU.mult))

            def low_qk(chunks):
                for n in chunks:
                    q_high.wait(eng, n)
                    k_low.done(vec.tensor_tensor(low_buffer(n), f32(low_buffer(n)), f32(high_buffer(n)),
                                                 ALU.subtract))

            def low_w(k):
                for i, (raw, kept) in enumerate(w_halves(k)):
                    w_high.wait(eng, 2 * k + i)
                    w_low.done(vec.tensor_tensor(kept(1), raw, f32(kept(0)), ALU.subtract))

            ln_stats(0)
            ln_recip(0)
            normalise(0)
            normalise(1)
            low_w(0)
            normalise(2)
            normalise(3)
            for t in range(GT):
                low_x(t)
            low_w(1)
            a_const.wait(eng, 0)
            ident_cast.done(vec.tensor_copy(ident_bf[:, :], ident[:, :]))
            for g in range(GROUPS):
                more = g + 1 < GROUPS
                t = GT * (g + 1)
                if more:
                    ln_stats(g + 1)
                    ln_recip(g + 1)
                    normalise(t)
                    normalise(t + 1)
                for p in range(4):
                    rope_products(g, p)
                    if more:
                        low_x(t + p)
                        if p < 2:
                            normalise(t + 2 + p)
                    if p < 2 and g:
                        scale_qk(g - 1, 4 + 2 * p)
                        scale_qk(g - 1, 5 + 2 * p)
                    if p < 2 and g == 0:
                        low_w(2 + p)
                    if p == 2 and g == 0:
                        for k in range(CHUNKS):
                            wv_high.wait(eng, k)
                            wv_low.done(vec.tensor_tensor(wv[:, 1, k, :], v_raw[:, k, :], f32(wv[:, 0, k, :]),
                                                          ALU.subtract))
                    if p == 2:
                        rms_recip(g, 0)
                for c in range(4):
                    scale_qk(g, c)
                if not more:
                    low_qk(LOW_DVE[:2])
                rms_recip(g, 1)
            def fill(h):
                if h == 0:
                    r_dev.wait(eng, 2 * GROUPS - 1)
                else:
                    maxed.wait(eng, PAIRS * h - 2)
                filled.done(vec.memset(psum[:, 0:2, 0:P], LOWEST))

            def merge(n):
                score.wait(eng, n)
                if n in M_TR:
                    m_tr.wait(eng, M_TR[n])
                if n in W_TR:
                    w_tr.wait(eng, W_TR[n])
                merged.done(vec.copy_predicated(psum[:, 2 * (n % 2):2 * (n % 2) + 2, 0:P], mask[:, :, :].bitcast(U32),
                                                psum[:, 2 * (n % 2):2 * (n % 2) + 2, 2 * P:3 * P]))

            def maximum(n):
                h, j = head_pair(n)
                slot = 2 * (n % 2)
                merged.wait(eng, n)
                if h >= 2:
                    m_low.wait(eng, 2 * (h - 2) + j // 4)
                if j == 0:
                    vec.tensor_reduce(neg_max[:, h % 2, 0:1], psum[:, slot, 0:P], axis=AX_X, op=ALU.max, negate=True)
                    maxed.done(vec.tensor_reduce(neg_max[:, h % 2, 1:2], psum[:, slot + 1, 0:2 * P], axis=AX_X,
                                                 op=ALU.max, negate=True))
                else:
                    maxed.done(vec.tensor_reduce(neg_max[:, h % 2, 2 * j:2 * j + 2], psum[:, slot:slot + 2, 0:2 * P],
                                                 axis=AX_X, op=ALU.max, negate=True))

            def split_maxima(c):
                h, half = divmod(c, 2)
                maxed.wait(eng, 4 * c + 3)
                if c >= 2:
                    m_tr.wait(eng, c - 2)
                cols = neg_max[:, h % 2, PAIRS * half:PAIRS * (half + 1)]
                m_high.done(vec.tensor_copy(max_split[:, c % 2, 0:PAIRS], cols))
                m_high.wait(eng, c)
                m_low.done(vec.tensor_tensor(max_split[:, c % 2, PAIRS:2 * PAIRS], cols,
                                             f32(max_split[:, c % 2, 0:PAIRS]), ALU.subtract))

            def evacuate_rows(c, s):
                m_tr.wait(eng, c)
                if c >= 2:
                    a_rows[c % 2].wait(eng, c // 2 - 1)
                m_row.done(vec.tensor_copy(max_rows[:, c % 2, :], psum[0:2 * PAIRS, 2 * (s % 2), 3 * P:4 * P]))

            def ternary_w(k, i):
                w, var, fold = stage_w[:, k % 2, 0:DIM], stage_w[:, k % 2, DIM:2 * DIM], w_fold[:, k % 2, :]
                if i == 0:
                    a_wraw2[k % 2].wait(eng, k // 2)
                    if k >= 2:
                        w_tr.wait(eng, 2 * (k - 2) + 1)
                w_tern.wait(eng, 4 * k + i - 1)
                if i == 0:
                    w_tern.done(vec.tensor_scalar(fold, w, TH_W, SC_W, ALU.is_gt, ALU.mult))
                elif i == 1:
                    w_tern.done(vec.tensor_scalar(w, w, -TH_W, SC_W, ALU.is_lt, ALU.mult))
                elif i == 2:
                    w_tern.done(vec.tensor_tensor(fold, fold, w, ALU.subtract))
                else:
                    w_tern.done(vec.tensor_tensor(fold, fold, var, ALU.add))

            def split_wf(i, s):
                k, d0 = i // 2, 2 * (i % 2)
                w_tr.wait(eng, i)
                for e in range(2):
                    src = psum[:, 2 * (s % 2) + e, 3 * P:4 * P]
                    high = wf[:, 0, d0 + e, P * k:P * (k + 1)]
                    wf_high.done(vec.tensor_scalar(high, src, SC_X, None, ALU.mult))
                    wf_high.wait(eng, 2 * i + e)
                    wf_low.done(vec.scalar_tensor_tensor(wf[:, 1, d0 + e, P * k:P * (k + 1)], src, SC_X, f32(high),
                                                         ALU.mult, ALU.subtract))

            def recip_sums(u):
                a_sums.wait(eng, u)
                a_recs.wait(eng, u - 2)
                recd.done(vec.reciprocal(recs[:, u % 2, :], sums[:, u % 2, :]))

            def divide(i):
                c, g = divmod(i, GROUPS)
                cols = slice(GROUP * g, GROUP * (g + 1))
                a_bc.wait(eng, i // 2)
                o_done.done(vec.tensor_tensor(o_t[:, c, cols], o_t[:, c, cols], rec_bc[:, cols], ALU.mult))

            def finish_projections(s):
                for c in ((4, 5), (6, 7))[s]:
                    scale_qk(GROUPS - 1, c)
                if s == 0:
                    low_qk(LOW_DVE[2:])

            late = GROUPS * CHUNKS - 2
            mask_set.wait(eng, 0)
            fill(0)
            finish_projections(0)
            for s in range(LAST):
                if s < STEPS:
                    merge(s)
                if s in M_TR:
                    evacuate_rows(M_TR[s], s)
                if s in W_TR:
                    split_wf(W_TR[s], s)
                if s < STEPS:
                    maximum(s)
                    if s % PAIRS == PAIRS - 2 and s // PAIRS + 1 < HEADS:
                        fill(s // PAIRS + 1)
                    if s % 4 == 3:
                        split_maxima(s // 4)
                if s in WO_S:
                    k = WO_S.index(s)
                    wo_high.wait(eng, k)
                    wo_low.done(vec.tensor_tensor(wo[:, 1, k, :], stage_w[:, k % 2, 0:DIM], f32(wo[:, 0, k, :]),
                                                  ALU.subtract))
                if s in TERN_OPS:
                    ternary_w(*TERN_OPS[s])
                if s in RECIP:
                    recip_sums(RECIP[s])
                if s in DIVIDE and DIVIDE[s] < late:
                    divide(DIVIDE[s])
                    if DIVIDE[s] == late - 1:
                        o_high.wait(eng, SPLIT_O.index(BY_DVE))
                        o_low_dve.done(vec.tensor_tensor(o_split[0][:, 1, CHUNKS - 1, :], o_t[:, CHUNKS - 1, 0:GROUP],
                                                         f32(o_split[0][:, 0, CHUNKS - 1, :]), ALU.subtract))
                if s == 5:
                    finish_projections(1)

            def residual(t):
                wo_mm.wait(eng, t)
                a_x3[t % 4].wait(eng, t // 4)
                if t >= 8:
                    out_s.wait(eng, t - 8)
                x1_s.done(vec.tensor_tensor(x1[:, t % 8, :], psum[:, BANK_WO + t % NWO, :], x3[:, t % 4, :], ALU.add))
                x1_s.wait(eng, t)
                bn3.done(vec.bn_stats(stats[:, t % 4, :], x1[:, t % 8, :]))
                bn3.wait(eng, t)
                y_s.wait(eng, t - 4)
                aggr3.done(vec.bn_aggr(mean_var[:, t % 4, :], stats[:, t % 4, :]))

            def quantise(t):
                dev3.wait(eng, t)
                y_s.wait(eng, t - 4)
                rstd3.done(vec.reciprocal(rstd[:, t % 4:t % 4 + 1], dev[:, t % 4:t % 4 + 1]))
                rstd3.wait(eng, t)
                y = y3[:, t % 2, :]
                y_s.done(vec.tensor_scalar(y, x1[:, t % 8, :], mean_var[:, t % 4, 0:1], rstd[:, t % 4:t % 4 + 1],
                                           ALU.subtract, ALU.mult))
                y_s.wait(eng, t)
                below_s.done(vec.tensor_scalar(below[:, t % 2, :], y, -TH_X, None, ALU.is_lt))
                below_s.wait(eng, t)
                xq_tr.wait(eng, t - 6)
                xq_s.done(vec.scalar_tensor_tensor(xq[:, t % 6, :], y, TH_X, below[:, t % 2, :], ALU.is_gt,
                                                   ALU.subtract))

            def result(t):
                ffn_mm.wait(eng, t)
                if t >= 4:
                    a_out[t % 4].wait(eng, t // 4 - 1)
                out_s.done(vec.tensor_tensor(out_stage[:, t % 4, :], psum[:, BANK_FFN + t % 2, :], x1[:, t % 8, :],
                                             ALU.add))

            for t in range(TILES + 6):
                if t < TILES:
                    residual(t)
                if 0 <= t - 1 < TILES:
                    quantise(t - 1)
                if 0 <= t - 6 < TILES:
                    result(t - 6)


def kernel(L0_attn_hidden_states, L0_attn_Wqkv, L0_attn_q_norm_w, L0_attn_k_norm_w, L0_attn_Wo, L0_ffn_weight,
           L0_ffn_rram_variation):
    import concourse.bacc as bacc
    from concourse.bass_utils import run_bass_kernel_spmd

    f4 = np.float32
    inv_freq = (f4(1.0) / np.power(f4(THETA), np.arange(0, HEAD_DIM, 2, dtype=f4) / f4(HEAD_DIM))).astype(f4)
    angle = (np.arange(SEQ, dtype=f4)[None, :] * inv_freq[:, None]).astype(f4).astype(np.float64)
    cos = np.tile(np.cos(angle).astype(f4), (P // HALF, 1))
    sin = np.tile(np.sin(angle).astype(f4), (P // HALF, 1))

    def by_chunk(w):
        return np.asarray(w).reshape(2, 8, 2, HALF).transpose(1, 3, 0, 2).reshape(P, CHUNKS)

    arrays = {
        "x": np.ascontiguousarray(np.asarray(L0_attn_hidden_states).reshape(SEQ, DIM)),
        "wqkv": np.ascontiguousarray(L0_attn_Wqkv),
        "qkw": np.ascontiguousarray(np.concatenate([by_chunk(L0_attn_q_norm_w), by_chunk(L0_attn_k_norm_w)], 1)),
        "wo": np.ascontiguousarray(L0_attn_Wo),
        "wf": np.ascontiguousarray(L0_ffn_weight),
        "rram": np.ascontiguousarray(L0_ffn_rram_variation),
        "cos": cos, "sin": sin, "ident": np.eye(P, dtype=f4),
    }
    nc = bacc.Bacc("TRN2", target_bir_lowering=False, num_devices=1)
    args = [nc.dram_tensor(f"in_{n}", a.shape, mybir.dt.from_np(a.dtype), kind="ExternalInput").ap()
            for n, a in arrays.items()]
    out = nc.dram_tensor("out", (SEQ, DIM), F32, kind="ExternalOutput").ap()
    build(nc, *args, out)
    result = run_bass_kernel_spmd(nc, [{f"in_{n}": a for n, a in arrays.items()}], core_ids=[0])
    return result.results[0]["out"].reshape(1, SEQ, DIM)
```
